# Optimizing a Trainium2 kernel written in Bass

```python
import numpy as np
import jax
import jax.numpy as jnp

def _softmax(x, axis=-1):
    return jax.nn.softmax(x, axis=axis)

def _gelu(x):
    return jax.nn.gelu(x, approximate=True)

def _silu(x):
    return jax.nn.silu(x)

def _sigmoid(x):
    return jax.nn.sigmoid(x)

def _layernorm(x, axis=-1, eps=1e-05):
    m = jnp.mean(x, axis=axis, keepdims=True)
    v = jnp.var(x, axis=axis, keepdims=True)
    return (x - m) / jnp.sqrt(v + eps)

def _scatter_add(tgt, idx, src, axis=0):
    return tgt.at[idx].add(src)

def _segment_sum(src, seg, n):
    return jax.ops.segment_sum(src, seg, n)
kernel_name = 'mk_macaron_d2_jaxref_r8_43f048'

def setup_inputs(seed: int=0):
    np.random.seed(seed)
    _w = jnp.asarray

    def _L0_attn_setup():
        import jax, jax.numpy as jnp
        import numpy as np
        DIM = 256
        HEADS = 16
        HEAD_DIM = DIM // HEADS
        RANK = 16
        ALPHA = 8.0
        SCALING = ALPHA / RANK
        SCALE = HEAD_DIM ** (-0.5)

        def lora_linear(x, W, b, Bm, Am):
            out = jnp.einsum('bld,od->blo', x, W) + b
            upd = jnp.einsum('blr,or->blo', jnp.einsum('bld,rd->blr', x, Bm), Am)
            return out + SCALING * upd

        def _split(t):
            B, L, D = t.shape
            return t.reshape(B, L, HEADS, HEAD_DIM).transpose(0, 2, 1, 3)
        key = jax.random.key(seed)
        ks = jax.random.split(key, 20)
        B, L = (4, 256)
        x = jax.random.normal(ks[0], (B, L, DIM), dtype=jnp.float32)
        s = 0.02
        inp = {'x': x}
        for i, name in enumerate(['q', 'k', 'v', 'o']):
            inp[f'W{name}'] = jax.random.normal(ks[1 + 4 * i], (DIM, DIM), jnp.float32) * s
            inp[f'b{name}'] = jax.random.normal(ks[2 + 4 * i], (DIM,), jnp.float32) * s
            inp[f'B{name}'] = jax.random.normal(ks[3 + 4 * i], (RANK, DIM), jnp.float32) * s
            inp[f'A{name}'] = jax.random.uniform(ks[4 + 4 * i], (DIM, RANK), jnp.float32, -0.1, 0.1)
        return inp
    _L0_attn_in = _L0_attn_setup()

    def _L0_ffn_setup():
        import jax, jax.numpy as jnp
        import numpy as np
        B, S, D_IN, D_OUT = (4, 256, 256, 256)
        E, R, TOP_K = (8, 8, 2)
        ALPHA = 16.0
        SCALE = ALPHA / R
        key = jax.random.key(seed)
        ks = jax.random.split(key, 6)
        x = jax.random.normal(ks[0], (B, S, D_IN), dtype=jnp.float32)
        W_base = jax.random.normal(ks[1], (D_OUT, D_IN), dtype=jnp.float32) / np.sqrt(D_IN)
        b_base = jax.random.normal(ks[2], (D_OUT,), dtype=jnp.float32) * 0.01
        W_router = jax.random.normal(ks[3], (E, D_IN), dtype=jnp.float32) / np.sqrt(D_IN)
        A_w = jax.random.normal(ks[4], (E, R, D_IN), dtype=jnp.float32) / np.sqrt(D_IN)
        B_w = jax.random.normal(ks[5], (E, D_OUT, R), dtype=jnp.float32) * 0.02
        return {'x': x, 'W_base': W_base, 'b_base': b_base, 'W_router': W_router, 'A_w': A_w, 'B_w': B_w}
    _L0_ffn_in = _L0_ffn_setup()

    def _L1_attn_setup():
        import jax, jax.numpy as jnp
        import numpy as np
        B, S, D, H = (2, 256, 256, 16)
        QR, KVR = (96, 64)
        DN, DR, DV = (128, 64, 128)
        EPS = 1e-06
        WSCALE = 0.02

        def rms_norm(x, w, eps=EPS):
            return x * jax.lax.rsqrt(jnp.mean(x * x, axis=-1, keepdims=True) + eps) * w

        def rope_cos_sin(seq_len, d):
            inv = 1.0 / 10000.0 ** (jnp.arange(0, d, 2, dtype=jnp.float32) / d)
            t = jnp.arange(seq_len, dtype=jnp.float32)
            f = jnp.outer(t, inv)
            return (jnp.cos(f)[:, None, :], jnp.sin(f)[:, None, :])

        def apply_rope(x, cos, sin):
            x1, x2 = (x[..., 0::2], x[..., 1::2])
            o1 = x1 * cos - x2 * sin
            o2 = x1 * sin + x2 * cos
            return jnp.stack([o1, o2], axis=-1).reshape(x.shape)
        key = jax.random.key(seed)
        ks = jax.random.split(key, 10)
        return {'x': jax.random.normal(ks[0], (B, S, D), jnp.float32), 'wq_down': jax.random.normal(ks[1], (D, QR), jnp.float32) * WSCALE, 'q_norm_w': jnp.ones((QR,), jnp.float32), 'wq_up': jax.random.normal(ks[2], (QR, H * DN), jnp.float32) * WSCALE, 'wq_rope': jax.random.normal(ks[3], (QR, H * DR), jnp.float32) * WSCALE, 'wkv_down': jax.random.normal(ks[4], (D, KVR), jnp.float32) * WSCALE, 'kv_norm_w': jnp.ones((KVR,), jnp.float32), 'wkv_up': jax.random.normal(ks[5], (KVR, H * (DN + DV)), jnp.float32) * WSCALE, 'wk_rope': jax.random.normal(ks[6], (D, DR), jnp.float32) * WSCALE, 'wo': jax.random.normal(ks[7], (H * DV, D), jnp.float32) * WSCALE}
    _L1_attn_in = _L1_attn_setup()

    def _L1_ffn_setup():
        import jax, jax.numpy as jnp
        import numpy as np
        B, S, H, I, E, K = (4, 512, 256, 128, 32, 4)
        key = jax.random.key(seed)
        k1, k2, k3, k4, k5, k6 = jax.random.split(key, 6)
        hidden_states = jax.random.normal(k1, (B, S, H), dtype=jnp.float32)
        topk_idx = jax.random.randint(k2, (B * S, K), 0, E)
        w = jax.random.uniform(k3, (B * S, K), dtype=jnp.float32)
        topk_weight = w / jnp.sum(w, axis=-1, keepdims=True)
        scale = 0.02
        gate_weight = jax.random.normal(k4, (E, I, H), dtype=jnp.float32) * scale
        up_weight = jax.random.normal(k5, (E, I, H), dtype=jnp.float32) * scale
        down_weight = jax.random.normal(k6, (E, H, I), dtype=jnp.float32) * scale
        return {'hidden_states': hidden_states, 'gate_weight': gate_weight, 'up_weight': up_weight, 'down_weight': down_weight, 'topk_idx': topk_idx, 'topk_weight': topk_weight}
    _L1_ffn_in = _L1_ffn_setup()
    _d = {'L0_attn_x': _L0_attn_in['x'], 'L0_attn_Wq': _L0_attn_in['Wq'], 'L0_attn_bq': _L0_attn_in['bq'], 'L0_attn_Bq': _L0_attn_in['Bq'], 'L0_attn_Aq': _L0_attn_in['Aq'], 'L0_attn_Wk': _L0_attn_in['Wk'], 'L0_attn_bk': _L0_attn_in['bk'], 'L0_attn_Bk': _L0_attn_in['Bk'], 'L0_attn_Ak': _L0_attn_in['Ak'], 'L0_attn_Wv': _L0_attn_in['Wv'], 'L0_attn_bv': _L0_attn_in['bv'], 'L0_attn_Bv': _L0_attn_in['Bv'], 'L0_attn_Av': _L0_attn_in['Av'], 'L0_attn_Wo': _L0_attn_in['Wo'], 'L0_attn_bo': _L0_attn_in['bo'], 'L0_attn_Bo': _L0_attn_in['Bo'], 'L0_attn_Ao': _L0_attn_in['Ao'], 'L0_ffn_W_base': _L0_ffn_in['W_base'], 'L0_ffn_b_base': _L0_ffn_in['b_base'], 'L0_ffn_W_router': _L0_ffn_in['W_router'], 'L0_ffn_A_w': _L0_ffn_in['A_w'], 'L0_ffn_B_w': _L0_ffn_in['B_w'], 'L1_attn_wq_down': _L1_attn_in['wq_down'], 'L1_attn_q_norm_w': _L1_attn_in['q_norm_w'], 'L1_attn_wq_up': _L1_attn_in['wq_up'], 'L1_attn_wq_rope': _L1_attn_in['wq_rope'], 'L1_attn_wkv_down': _L1_attn_in['wkv_down'], 'L1_attn_kv_norm_w': _L1_attn_in['kv_norm_w'], 'L1_attn_wkv_up': _L1_attn_in['wkv_up'], 'L1_attn_wk_rope': _L1_attn_in['wk_rope'], 'L1_attn_wo': _L1_attn_in['wo'], 'L1_ffn_gate_weight': _L1_ffn_in['gate_weight'], 'L1_ffn_up_weight': _L1_ffn_in['up_weight'], 'L1_ffn_down_weight': _L1_ffn_in['down_weight'], 'L1_ffn_topk_idx': _L1_ffn_in['topk_idx'], 'L1_ffn_topk_weight': _L1_ffn_in['topk_weight']}
    _x0 = _d['L0_attn_x']
    _d['L0_attn_x'] = jax.random.normal(jax.random.fold_in(jax.random.key(seed), 1), (4, 512, 256), dtype=_x0.dtype)
    del _x0
    return _d

def reference(L0_attn_x, L0_attn_Wq, L0_attn_bq, L0_attn_Bq, L0_attn_Aq, L0_attn_Wk, L0_attn_bk, L0_attn_Bk, L0_attn_Ak, L0_attn_Wv, L0_attn_bv, L0_attn_Bv, L0_attn_Av, L0_attn_Wo, L0_attn_bo, L0_attn_Bo, L0_attn_Ao, L0_ffn_W_base, L0_ffn_b_base, L0_ffn_W_router, L0_ffn_A_w, L0_ffn_B_w, L1_attn_wq_down, L1_attn_q_norm_w, L1_attn_wq_up, L1_attn_wq_rope, L1_attn_wkv_down, L1_attn_kv_norm_w, L1_attn_wkv_up, L1_attn_wk_rope, L1_attn_wo, L1_ffn_gate_weight, L1_ffn_up_weight, L1_ffn_down_weight, L1_ffn_topk_idx, L1_ffn_topk_weight):

    def _L0_attn_ref(x, Wq, bq, Bq, Aq, Wk, bk, Bk, Ak, Wv, bv, Bv, Av, Wo, bo, Bo, Ao):
        import jax, jax.numpy as jnp
        import numpy as np
        DIM = 256
        HEADS = 16
        HEAD_DIM = DIM // HEADS
        RANK = 16
        ALPHA = 8.0
        SCALING = ALPHA / RANK
        SCALE = HEAD_DIM ** (-0.5)

        def lora_linear(x, W, b, Bm, Am):
            out = jnp.einsum('bld,od->blo', x, W) + b
            upd = jnp.einsum('blr,or->blo', jnp.einsum('bld,rd->blr', x, Bm), Am)
            return out + SCALING * upd

        def _split(t):
            B, L, D = t.shape
            return t.reshape(B, L, HEADS, HEAD_DIM).transpose(0, 2, 1, 3)
        q = _split(lora_linear(x, Wq, bq, Bq, Aq))
        k = _split(lora_linear(x, Wk, bk, Bk, Ak))
        v = _split(lora_linear(x, Wv, bv, Bv, Av))
        scores = jnp.einsum('bhqd,bhkd->bhqk', q, k) * SCALE
        attn = jax.nn.softmax(scores, axis=-1)
        out = jnp.einsum('bhqk,bhkd->bhqd', attn, v)
        B, H, L, hd = out.shape
        out = out.transpose(0, 2, 1, 3).reshape(B, L, H * hd)
        return lora_linear(out, Wo, bo, Bo, Ao)

    def _L0_ffn_ref(x, W_base, b_base, W_router, A_w, B_w):
        import jax, jax.numpy as jnp
        import numpy as np
        B, S, D_IN, D_OUT = (4, 256, 256, 256)
        E, R, TOP_K = (8, 8, 2)
        ALPHA = 16.0
        SCALE = ALPHA / R
        y = jnp.einsum('bsd,od->bso', x, W_base) + b_base
        logits = jnp.einsum('bsd,ed->bse', x, W_router)
        topk_vals, topk_idx = jax.lax.top_k(logits, TOP_K)
        gates = jax.nn.softmax(topk_vals, axis=-1)
        h = jnp.einsum('bsd,erd->bser', x, A_w)
        expert_outs = jnp.einsum('bser,eor->bseo', h, B_w) * SCALE
        topk_outs = jnp.take_along_axis(expert_outs, topk_idx[..., None], axis=2)
        fused = jnp.sum(topk_outs * gates[..., None], axis=2)
        return y + fused

    def _L1_attn_ref(x, wq_down, q_norm_w, wq_up, wq_rope, wkv_down, kv_norm_w, wkv_up, wk_rope, wo):
        import jax, jax.numpy as jnp
        import numpy as np
        B, S, D, H = (2, 256, 256, 16)
        QR, KVR = (96, 64)
        DN, DR, DV = (128, 64, 128)
        EPS = 1e-06
        WSCALE = 0.02

        def rms_norm(x, w, eps=EPS):
            return x * jax.lax.rsqrt(jnp.mean(x * x, axis=-1, keepdims=True) + eps) * w

        def rope_cos_sin(seq_len, d):
            inv = 1.0 / 10000.0 ** (jnp.arange(0, d, 2, dtype=jnp.float32) / d)
            t = jnp.arange(seq_len, dtype=jnp.float32)
            f = jnp.outer(t, inv)
            return (jnp.cos(f)[:, None, :], jnp.sin(f)[:, None, :])

        def apply_rope(x, cos, sin):
            x1, x2 = (x[..., 0::2], x[..., 1::2])
            o1 = x1 * cos - x2 * sin
            o2 = x1 * sin + x2 * cos
            return jnp.stack([o1, o2], axis=-1).reshape(x.shape)
        bs, seq_len, _ = x.shape
        qc = rms_norm(x @ wq_down, q_norm_w)
        q_nope = (qc @ wq_up).reshape(bs, seq_len, H, DN)
        q_pe = (qc @ wq_rope).reshape(bs, seq_len, H, DR)
        kvc = rms_norm(x @ wkv_down, kv_norm_w)
        kv = (kvc @ wkv_up).reshape(bs, seq_len, H, DN + DV)
        k_nope, v = (kv[..., :DN], kv[..., DN:])
        k_rope = (x @ wk_rope).reshape(bs, seq_len, 1, DR)
        cos, sin = rope_cos_sin(seq_len, DR)
        q_pe = apply_rope(q_pe, cos, sin)
        k_rope = apply_rope(k_rope, cos, sin)
        k_rope = jnp.broadcast_to(k_rope, (bs, seq_len, H, DR))
        q = jnp.concatenate([q_nope, q_pe], axis=-1)
        k = jnp.concatenate([k_nope, k_rope], axis=-1)
        scale = 1.0 / np.sqrt(DN + DR).astype(np.float32)
        scores = jnp.einsum('bqhd,bkhd->bhqk', q, k) * scale
        mask = jnp.triu(jnp.full((seq_len, seq_len), -jnp.inf, jnp.float32), k=1)
        probs = jax.nn.softmax(scores.astype(jnp.float32) + mask, axis=-1).astype(q.dtype)
        out = jnp.einsum('bhqk,bkhd->bqhd', probs, v).reshape(bs, seq_len, H * DV)
        return out @ wo

    def _L1_ffn_ref(hidden_states, gate_weight, up_weight, down_weight, topk_idx, topk_weight):
        import jax, jax.numpy as jnp
        import numpy as np
        B, S, H, I, E, K = (4, 512, 256, 128, 32, 4)
        b, s, h = hidden_states.shape
        n_experts = gate_weight.shape[0]
        top_k = topk_idx.shape[-1]
        x = hidden_states.reshape(-1, h)
        n = x.shape[0]
        flat_expert = topk_idx.reshape(-1)
        flat_weight = topk_weight.reshape(-1)
        perm = jnp.argsort(flat_expert)
        tok_sorted = jnp.repeat(jnp.arange(n), top_k)[perm]
        group_sizes = jnp.bincount(flat_expert, length=n_experts).astype(jnp.int32)
        xs = x[tok_sorted]
        g = jax.lax.ragged_dot(xs, jnp.swapaxes(gate_weight, 1, 2), group_sizes)
        u = jax.lax.ragged_dot(xs, jnp.swapaxes(up_weight, 1, 2), group_sizes)
        hmid = jax.nn.silu(g) * u
        o = jax.lax.ragged_dot(hmid, jnp.swapaxes(down_weight, 1, 2), group_sizes)
        o = o * flat_weight[perm][:, None]
        y = jnp.zeros((n, h), dtype=x.dtype).at[tok_sorted].add(o)
        return y.reshape(b, s, h)
    x = L0_attn_x
    x = x + 0.5 * _L0_ffn_ref(_layernorm(x, axis=-1), L0_ffn_W_base, L0_ffn_b_base, L0_ffn_W_router, L0_ffn_A_w, L0_ffn_B_w)
    x = x + _L0_attn_ref(_layernorm(x, axis=-1), L0_attn_Wq, L0_attn_bq, L0_attn_Bq, L0_attn_Aq, L0_attn_Wk, L0_attn_bk, L0_attn_Bk, L0_attn_Ak, L0_attn_Wv, L0_attn_bv, L0_attn_Bv, L0_attn_Av, L0_attn_Wo, L0_attn_bo, L0_attn_Bo, L0_attn_Ao)
    x = x + 0.5 * _L0_ffn_ref(_layernorm(x, axis=-1), L0_ffn_W_base, L0_ffn_b_base, L0_ffn_W_router, L0_ffn_A_w, L0_ffn_B_w)
    x = x + 0.5 * _L1_ffn_ref(_layernorm(x, axis=-1), L1_ffn_gate_weight, L1_ffn_up_weight, L1_ffn_down_weight, L1_ffn_topk_idx, L1_ffn_topk_weight)
    x = x + _L1_attn_ref(_layernorm(x, axis=-1), L1_attn_wq_down, L1_attn_q_norm_w, L1_attn_wq_up, L1_attn_wq_rope, L1_attn_wkv_down, L1_attn_kv_norm_w, L1_attn_wkv_up, L1_attn_wk_rope, L1_attn_wo)
    x = x + 0.5 * _L1_ffn_ref(_layernorm(x, axis=-1), L1_ffn_gate_weight, L1_ffn_up_weight, L1_ffn_down_weight, L1_ffn_topk_idx, L1_ffn_topk_weight)
    return x

_drawn_inputs = setup_inputs


def setup_inputs(seed=0):
    import zlib

    import numpy as np

    out = dict(_drawn_inputs(seed))
    spreads = {'L1_attn_q_norm_w': (1.0, 0.6), 'L1_attn_kv_norm_w': (1.0, 0.6)}
    factors = {'L0_attn_Wq': 8.0,
     'L0_attn_bq': 8.0,
     'L0_attn_Bq': 8.0,
     'L0_attn_Aq': 8.0,
     'L0_attn_Wk': 8.0,
     'L0_attn_bk': 64.0,
     'L0_attn_Bk': 8.0,
     'L0_attn_Ak': 8.0,
     'L0_attn_Wv': 8.0,
     'L0_attn_bv': 8.0,
     'L0_attn_Bv': 8.0,
     'L0_attn_Av': 8.0,
     'L0_attn_Wo': 8.0,
     'L0_attn_bo': 17.679,
     'L0_attn_Bo': 8.0,
     'L0_attn_Ao': 8.0,
     'L0_ffn_b_base': 7.568,
     'L1_attn_wq_down': 8.0,
     'L1_attn_wq_up': 8.0,
     'L1_attn_wq_rope': 8.0,
     'L1_attn_wkv_down': 4.671,
     'L1_attn_wkv_up': 4.653,
     'L1_attn_wk_rope': 8.0,
     'L1_attn_wo': 4.775,
     'L1_ffn_gate_weight': 8.0,
     'L1_ffn_up_weight': 8.0,
     'L1_ffn_down_weight': 8.0,
     'L1_ffn_topk_weight': 8.0}
    for name, (base, spread) in spreads.items():
        noise = np.random.default_rng([zlib.crc32(name.encode()), seed]).standard_normal(out[name].shape)
        drawn = base * np.exp(spread * noise) if base else spread * noise
        out[name] = jnp.asarray(drawn.astype(out[name].dtype))
    for name, factor in factors.items():
        out[name] = (out[name] * factor).astype(out[name].dtype)
    return out
```

```python
from contextlib import ExitStack

import numpy as np

import concourse.bass as bass
from concourse import mybir

F32 = mybir.dt.float32
BF16 = mybir.dt.bfloat16
I32 = mybir.dt.int32
U32 = mybir.dt.uint32
ALU = mybir.AluOpType
ACT = mybir.ActivationFunctionType
AX = mybir.AxisListType.X
ds = bass.ds

P = 128
B, L, D = 4, 512, 256
TILES = B * L // P
TPB = L // P
KD = D // P


class Link:

    def __init__(self, eng, sem, tick=None):
        self.eng, self.sem, self.base, self.n, self.tick = eng, sem, 0, 0, tick

    def body(self, base):
        self.base, self.n = base, 0

    def __call__(self, ins):
        self.n += 1
        ins.then_inc(self.sem, 1)
        self.eng.wait_ge(self.sem, self.base + self.n)
        if self.tick is not None:
            stand(self.eng, self.tick)


def stand(eng, tick):
    eng.sem_inc(tick, 1)


def inverse_root(dve, link, v, y, t):
    link(dve.tensor_scalar(t.bitcast(I32), v.bitcast(I32), 1, None, ALU.logical_shift_right))
    link(dve.tensor_scalar(y.bitcast(I32), t.bitcast(I32), -1.0, float(0x5F3759DF), ALU.mult, ALU.add))
    for _ in range(3):
        link(dve.scalar_tensor_tensor(out=t, in0=y, scalar=-0.5, in1=y, op0=ALU.mult, op1=ALU.mult))
        link(dve.tensor_tensor(t, t, v, ALU.mult))
        link(dve.scalar_tensor_tensor(out=y, in0=t, scalar=1.5, in1=y, op0=ALU.add, op1=ALU.mult))


def row_scales(dve, link, r):
    for t in range(TILES):
        ins = dve.bn_aggr(r.mv[:, 2 * t:2 * t + 2], r.stats[:, 6 * t:6 * t + 6])
    link(ins)
    var = r.mv[:, :].rearrange("p (j c) -> p j c", c=2)[:, :, 1]
    link(dve.tensor_scalar(r.var[:, :], var, 1e-5, None, ALU.add))
    inverse_root(dve, link, r.var[:, :], r.rstd[:, :], r.tmp[:, :])


def clear_after(ctx, nc, sems):
    def clear():
        with nc.Block() as block:
            @block.sync
            def _(sp):
                for s in sems:
                    sp.sem_clear(s)

    ctx.callback(clear)


def layernorm(dve, r, b, xn, xn_ready):
    for j in range(TPB):
        t = b * TPB + j
        dve.tensor_scalar(xn[:, j * D:(j + 1) * D], r.x[:, ds(t * D, D)], r.mv[:, ds(2 * t, 1)],
                          r.rstd[:, ds(t, 1)], ALU.subtract, ALU.mult).then_inc(xn_ready, 1)


def row_stats(dve, r, b):
    for j in range(TPB):
        t = b * TPB + j
        ins = dve.bn_stats(r.stats[:, ds(6 * t, 6)], r.x[:, ds(t * D, D)])
    return ins


class Rows:

    def __init__(self, ctx, nc):
        def sb(n, cols):
            return ctx.enter_context(nc.sbuf_tensor(n, [P, cols], F32))

        self.x, self.stats, self.mv = sb("x", TILES * D), sb("x_stats", 6 * TILES), sb("x_mv", 2 * TILES)
        self.var, self.rstd, self.tmp = sb("x_var", TILES), sb("x_rstd", TILES), sb("x_tmp", TILES)


def ffn_stage(nc, tag, r, ident, w):
    E, R = 8, 8
    NM = D + E + E * R
    wmain, wb, iota8 = w
    x = r.x
    with ExitStack() as ctx:
        def sb(n, shape, dt=F32):
            return ctx.enter_context(nc.sbuf_tensor(f"{tag}_{n}", shape, dt))

        def ps(n, cols):
            return ctx.enter_context(nc.psum_tensor(f"{tag}_{n}", [P, cols], F32))

        sems = []

        def sem(n):
            sems.append(ctx.enter_context(nc.semaphore(f"{tag}_{n}")))
            return sems[-1]

        xn, xT = sb("xn", [P, TPB * D]), sb("xT", [P, TPB * D])
        top, topi, idxf = sb("top", [P, 32]), sb("topi", [P, 32], U32), sb("idxf", [P, 32])
        gap, ex, den, g1, g2 = (sb(n, [P, 4]) for n in ("gap", "ex", "den", "g1", "g2"))
        oh, G = sb("oh", [P, 32]), sb("G", [P, 32])
        h, hT = sb("h", [P, TPB * E * R]), sb("hT", [E * R + 1, L])
        psM = [ps(f"psM{j}", 512) for j in range(4)]
        psT = [ps(f"psT{j}", 512) for j in range(2)]
        psG, psB = ps("psG", 512), ps("psB", 512)
        xn_ready, turned, xT_ready, main_done = (sem(n) for n in (
            "xn_ready", "turned", "xT_ready", "main_done"))
        main_read, h_copied, gap_ready, ex_ready, h_gated = (sem(n) for n in (
            "main_read", "h_copied", "gap_ready", "ex_ready", "h_gated"))
        h_turned, hT_ready, lora_done, lora_read, dstep, ones_set, turn_read = (sem(n) for n in (
            "h_turned", "hT_ready", "lora_done", "lora_read", "dstep", "ones_set", "turn_read"))
        ptick, vtick = sem("ptick"), sem("vtick")
        clear_after(ctx, nc, sems)
        block = ctx.enter_context(nc.Block())

        @block.tensor
        def _(pe):
            def base_and_router(b):
                for j in range(TPB + 1):
                    if j < TPB:
                        pe.wait_ge(xn_ready, b * 4 + j + 1)
                        pe.wait_ge(xT_ready, b * 4 + max(j - 1, 0))
                        for k in range(KD):
                            ins = pe.transpose(psT[j % 2][:, k * P:(k + 1) * P],
                                               xn[:, j * D + k * P:j * D + (k + 1) * P], ident[:, :])
                        ins.then_inc(turned, 1)
                    if j >= 1:
                        m = j - 1
                        pe.wait_ge(xT_ready, b * 4 + m + 1)
                        pe.wait_ge(h_copied, 4 * b)
                        for k in range(KD):
                            ins = pe.matmul(psM[m][:, 0:NM], xT[:, m * D + k * P:m * D + (k + 1) * P],
                                            wmain[:, k * NM:(k + 1) * NM], start=(k == 0), stop=(k == KD - 1))
                        ins.then_inc(main_done, 1)

            def lora(b):
                pe.wait_ge(h_gated, 1 + b + 1)
                pe.wait_ge(lora_read, 1 + b * 2)
                stand(pe, ptick)
                for j in range(TPB):
                    ins = pe.transpose(psG[0:64, j * P:(j + 1) * P], h[:, j * 64:(j + 1) * 64], ident[:, :])
                ins.then_inc(h_turned, 1)
                pe.wait_ge(hT_ready, b + 1)
                for j in range(TPB):
                    ins = pe.matmul((psB, psG)[j // 2][:, (j % 2) * D:(j % 2 + 1) * D], hT[:, j * P:(j + 1) * P],
                                    wb[0:65, 0:D], start=True, stop=True)
                    if j % 2:
                        ins.then_inc(lora_done, 1)

            pe.sem_inc(h_turned, 1)
            pe.wait_ge(ones_set, 1)
            base_and_router(0)
            with pe.Fori(0, B - 1) as b:
                base_and_router(b + 1)
                lora(b)
            lora(B - 1)

        @block.scalar
        def _(act):
            def turn(b):
                for j in range(TPB):
                    act.wait_ge(turned, b * 4 + j + 1)
                    act.wait_ge(main_done, b * 4)
                    act.copy(xT[:, j * D:(j + 1) * D], psT[j % 2][:, 0:D]).then_inc(xT_ready, 1)

            def rows(b):
                act.wait_ge(h_gated, 1 + b)
                act.wait_ge(h_turned, 1 + b)
                for j in range(TPB):
                    act.wait_ge(main_read, b * 4 + j + 1)
                    act.copy(h[:, j * 64:(j + 1) * 64], psM[j][:, D + E:NM]).then_inc(h_copied, 1)

            def gates(b):
                act.wait_ge(gap_ready, b + 1)
                act.activation(ex[:, :], gap[:, :], ACT.Exp).then_inc(ex_ready, 1)
                act.wait_ge(h_turned, 1 + b + 1)
                act.copy(hT[0:64, :], psG[0:64, :]).then_inc(hT_ready, 1)

            turn(0)
            with act.Fori(0, B - 1) as b:
                rows(b)
                turn(b + 1)
                gates(b)
            rows(B - 1)
            gates(B - 1)

        @block.vector
        def _(dve):
            link = Link(dve, dstep)
            NL = 11
            v3 = lambda t, c: t.rearrange("p (j c) -> p j c", c=c)

            def ln(b):
                dve.wait_ge(turned, b * TPB)
                layernorm(dve, r, b, xn, xn_ready)

            def gate(b):
                for j in range(TPB):
                    dve.wait_ge(main_done, b * 4 + j + 1)
                    stand(dve, vtick)
                    ins = dve.max(top[:, 8 * j:8 * j + 8], psM[j][:, D:D + E])
                link(ins)
                for j in range(TPB):
                    xj = x[:, ds((b * 4 + j) * D, D)]
                    dve.scalar_tensor_tensor(out=xj, in0=psM[j][:, 0:D], scalar=0.5, in1=xj, op0=ALU.mult, op1=ALU.add)
                    ins = dve.max_index(topi[:, 8 * j:8 * j + 8], top[:, 8 * j:8 * j + 8], psM[j][:, D:D + E])
                    ins.then_inc(main_read, 1)
                link(dve.tensor_tensor(gap[:, :], v3(top[:, :], 8)[:, :, 1], v3(top[:, :], 8)[:, :, 0], ALU.subtract))
                dve.sem_inc(gap_ready, 1)
                link(dve.tensor_copy(idxf[:, :], topi[:, :]))
                dve.wait_ge(ex_ready, b + 1)
                link(dve.tensor_scalar(den[:, :], ex[:, :], 1.0, None, ALU.add))
                link(dve.reciprocal(g1[:, :], den[:, :]))
                link(dve.tensor_tensor(g2[:, :], ex[:, :], g1[:, :], ALU.mult))
                io = iota8[:, 0:E].unsqueeze(1).to_broadcast([P, 4, E])
                for c, g, out in ((0, g1, G), (1, g2, oh)):
                    ic = v3(idxf[:, :], 8)[:, :, c:c + 1].to_broadcast([P, 4, E])
                    gc = g[:, :].unsqueeze(2).to_broadcast([P, 4, E])
                    link(dve.tensor_tensor(v3(out[:, :], 8), io, ic, ALU.is_equal))
                    link(dve.tensor_tensor(v3(out[:, :], 8), v3(out[:, :], 8), gc, ALU.mult))
                link(dve.tensor_tensor(G[:, :], G[:, :], oh[:, :], ALU.add))
                dve.wait_ge(h_copied, 4 * b + 4)
                hv = h[:, :].rearrange("p (g r) -> p g r", r=R)
                ins = dve.tensor_tensor(hv, hv, G[:, :].unsqueeze(2).to_broadcast([P, 32, R]), ALU.mult)
                ins.then_inc(h_gated, 1)

            def add(b):
                for c, out in enumerate((psB, psG)):
                    dve.wait_ge(lora_done, b * 2 + c + 1)
                    xj = x[:, ds((b * 4 + 2 * c) * D, 2 * D)]
                    dve.tensor_tensor(xj, out[:, :], xj, ALU.add).then_inc(lora_read, 1)
                dve.wait_ge(lora_read, 1 + b * 2 + 2)
                row_stats(dve, r, b)

            dve.memset(hT[64:65, :], 1.0).then_inc(ones_set, 1)
            dve.sem_inc(lora_read, 1)
            dve.sem_inc(h_gated, 1)
            row_scales(dve, link, r)
            ln(0)
            first = link.n
            with dve.Fori(0, B - 1) as b:
                link.body(first + b * NL)
                ln(b + 1)
                gate(b)
                add(b)
                assert link.n == NL, link.n
            link.body(first + (B - 1) * NL)
            gate(B - 1)
            add(B - 1)


def split3(pool, step, src, rest, hi, mid, lo, done):
    step(pool.tensor_copy(hi, src))
    step(pool.tensor_tensor(rest, src, hi, ALU.subtract))
    step(pool.tensor_copy(mid, rest))
    pool.tensor_tensor(lo, rest, mid, ALU.subtract).then_inc(done, 1)


def attention_stage(nc, r, ident, ring, wt, lora_b, lora_a, bias_qk, bias_v, bias_o, part_dram, max_dram):
    H, HD = 16, 16
    HPG, NG = 4, 4
    Q_PART, K_PART = (0, 0, 1, 1, 0, 2), (0, 1, 0, 1, 2, 0)
    NT = len(Q_PART) * HD
    KC = NT + 3
    SLOT = H * L
    x = r.x
    with ExitStack() as ctx:
        def sb(n, shape, dt=F32):
            return ctx.enter_context(nc.sbuf_tensor(f"a0_{n}", shape, dt))

        def ps(n, cols):
            return ctx.enter_context(nc.psum_tensor(f"a0_{n}", [P, cols], F32))

        def sem(n):
            return ctx.enter_context(nc.semaphore(f"a0_{n}"))

        QS = ring[:, 0:3 * SLOT // 2].bitcast(BF16)
        KS = ring[:, 3 * SLOT // 2:3 * SLOT].bitcast(BF16)
        xn, xT = sb("xn", [P, TPB * D]), sb("xT", [P, KD * L])
        qf, rest, part = sb("qf", [P, 2 * L]), sb("rest", [P, L]), sb("part", [P, 2 * 3 * L], BF16)
        V, VG = sb("V", [P, 3 * TPB * H * 32]), sb("VG", [P, TPB * HPG * 32])
        Pr = sb("P", [P, 2 * HPG * L])
        mx, nm, nrest, mpart = sb("mx", [P, 64]), sb("nm", [64, P]), sb("nrest", [64, P]), sb("mpart", [64, 3 * P], BF16)
        Osb, AO, rec = sb("Osb", [P, L]), sb("AO", [P, TPB * D]), sb("rec", [P, 16])
        AOT = xT
        psU = [ps(f"psU{i}", 512) for i in range(2)]
        psS = [ps(f"psS{i}", 1024) for i in range(2)]
        psO, psT = ps("psO", 512), ps("psT", 512)
        (dstep, pstep, u_ready, u_free, t_ready, t_free, xn_ready, exp_done, scored, pv_done, v_staged, o_copied,
         qf_ready, qf_free, part_ready, part_saved, terms_in, nm_ready, mpart_ready, max_saved, max_in, v_ready,
         ones_set, biased, w_ready, part_free, o_read, max_found, ptick) = (sem(n) for n in (
             "dstep", "pstep", "u_ready", "u_free", "t_ready", "t_free", "xn_ready", "exp_done", "scored", "pv_done",
             "v_staged", "o_copied", "qf_ready", "qf_free", "part_ready", "part_saved", "terms_in", "nm_ready",
             "mpart_ready", "max_saved", "max_in", "v_ready", "ones_set", "biased", "w_ready", "part_free", "o_read", "max_found", "ptick"))
        block = ctx.enter_context(nc.Block())

        def units(i):
            return sum(units_in(m) for m in range(-1, i))

        def units_in(i):
            return 8 * (i + 1 < B) + 64 * (0 <= i < B) + 4 * (i >= 1)

        def turns(i):
            return sum(turns_in(m) for m in range(-1, i))

        def turns_in(i):
            return 2 * (i + 1 < B) + 4 * (i >= 1) + (0 <= i < B) + 2 * (i >= 1)

        W8 = 8

        @block.sync
        def _(sp):
            for i in range(-1, B):
                s = i + 1
                if s < B:
                    for c in range(4):
                        sp.wait_ge(part_ready, 4 * s + c + 1)
                        sp.dma_start(part_dram[s, c // 2, :, (c % 2) * P:(c % 2 + 1) * P, :].rearrange("t p q -> p t q"),
                                     part[:, (c % 2) * 3 * L:(c % 2 + 1) * 3 * L].rearrange("p (t q) -> p t q", t=3)
                                     ).then_inc(part_saved, 16)
                        sp.wait_ge(part_saved, 16 * (4 * s + c + 1))
                        sp.sem_inc(part_free, 1)
                    if s >= 3:
                        sp.wait_ge(pv_done, 2 + 16 * (s - 2))
                    for dst, which, order in ((QS, 0, Q_PART), (KS, 1, K_PART)):
                        for t, c in enumerate(order):
                            sp.dma_start(dst[HD * t:HD * t + HD, (s % 3) * SLOT:(s % 3 + 1) * SLOT].rearrange(
                                "d (h q) -> d h q", h=H), part_dram[s, which, c, :, :].rearrange("(h d) q -> d h q", d=HD)
                                ).then_inc(terms_in, 16)
                if 0 <= i:
                    sp.wait_ge(mpart_ready, i + 1)
                    sp.dma_start(max_dram[i].rearrange("t p q -> p t q"),
                                 mpart[:, :].rearrange("p (t q) -> p t q", t=3)).then_inc(max_saved, 16)
                    sp.wait_ge(max_saved, 16 * (i + 1))
                    sp.dma_start(QS[NT:KC, (i % 3) * SLOT:(i % 3 + 1) * SLOT],
                                 max_dram[i].rearrange("t p q -> t (p q)")).then_inc(max_in, 16)

        @block.gpsimd
        def _(pool):
            step = Link(pool, pstep, ptick)
            step(pool.memset(VG[:, :], 0.0))
            step(pool.memset(V[:, :], 0.0))
            vv = V[:, :].rearrange("p (a c) -> p a c", c=32)
            step(pool.memset(KS[NT:KC, :], 1.0))
            pool.memset(vv[:, :, HD:HD + 1], 1.0).then_inc(ones_set, 1)
            vg = VG[:, :].rearrange("p (k a) -> p k a", k=TPB)

            def stage_v(i, g):
                pool.wait_ge(pv_done, 2 + 4 * ((i - 1) * NG + g))
                stand(pool, ptick)
                sl = ((i - 1) % 3) * TPB * H * 32
                src = V[:, sl:sl + TPB * H * 32].rearrange("p (k a) -> p k a", k=TPB)
                pool.tensor_copy(vg, src[:, :, ds(g * HPG * 32, HPG * 32)]).then_inc(v_staged, 1)

            for i in range(-1, B + 1):
                s = i + 1
                if s < B:
                    pool.wait_ge(xn_ready, 4 * s + 4)
                    for j in range(TPB):
                        xj = x[:, (s * TPB + j) * D:(s * TPB + j + 1) * D]
                        pool.tensor_tensor(xj, xj, bias_o, ALU.add).then_inc(biased, 1)
                    if i >= 1:
                        pool.wait_ge(v_ready, i)
                        stage_v(i, 0)
                    for c in range(4):
                        pool.wait_ge(qf_ready, 4 * s + c + 1)
                        pool.wait_ge(part_free, 4 * s + c - 1 if 4 * s + c >= 2 else 0)
                        o = (c % 2) * 3 * L
                        split3(pool, step, qf[:, (c % 2) * L:(c % 2 + 1) * L], rest[:, :], part[:, o:o + L],
                               part[:, o + L:o + 2 * L], part[:, o + 2 * L:o + 3 * L], part_ready)
                        pool.wait_ge(part_ready, 4 * s + c + 1)
                        pool.sem_inc(qf_free, 1)
                elif i >= 1:
                    pool.wait_ge(v_ready, i)
                    stage_v(i, 0)
                if i >= 1:
                    with pool.Fori(1, NG) as g:
                        stage_v(i, g)
                if 0 <= i < B:
                    pool.wait_ge(nm_ready, i + 1)
                    pool.wait_ge(max_saved, 16 * i)
                    split3(pool, step, nm[:, :], nrest[:, :], mpart[:, 0:P], mpart[:, P:2 * P], mpart[:, 2 * P:3 * P],
                           mpart_ready)

        @block.scalar
        def _(act):
            act.sem_inc(o_copied, 1)
            act.sem_inc(exp_done, 2)

            def exps(i, g):
                for kt in range(TPB):
                    st = (i - 1) * 16 + g * 4 + kt
                    act.wait_ge(pv_done, st + 1)
                    for u in range(2):
                        act.wait_ge(scored, 2 * st + u + 1)
                        o = ((kt % 2) * 4 + u * 2) * L
                        act.activation(Pr[:, o:o + 2 * L], psS[u][:, :], ACT.Exp).then_inc(exp_done, 1)
                act.wait_ge(pv_done, 2 + (i - 1) * 16 + g * 4 + 4)
                act.wait_ge(t_ready, g + (turns(i) + 2 * (i + 1 < B)))
                act.copy(Osb[:, :], psO[:, :]).then_inc(o_copied, 1)

            for i in range(-1, B + 1):
                if i + 1 < B:
                    for k in range(KD):
                        act.wait_ge(t_ready, turns(i) + k + 1)
                        if i >= 0:
                            act.wait_ge(u_ready, W8 + units(i))
                        act.copy(xT[:, k * L:(k + 1) * L], psT[:, :]).then_inc(t_free, 1)
                if i >= 1:
                    with act.Fori(0, NG) as g:
                        exps(i, g)
                n = turns(i) + 2 * (i + 1 < B) + 4 * (i >= 1)
                if 0 <= i < B:
                    act.wait_ge(t_ready, n + 1)
                    if i >= 1:
                        act.wait_ge(mpart_ready, i)
                    act.mul(nm[:, :], psT[0:64, 0:P], -1.0).then_inc(t_free, 1)
                    act.wait_ge(t_free, 1 + n + 1)
                    act.sem_inc(nm_ready, 1)
                    n += 1
                if i >= 1:
                    for k in range(KD):
                        act.wait_ge(t_ready, n + k + 1)
                        act.copy(AOT[:, k * L:(k + 1) * L], psT[:, :]).then_inc(t_free, 1)

        @block.vector
        def _(dve):
            link = Link(dve, dstep)
            dve.sem_inc(u_free, 2)
            dve.sem_inc(t_free, 1)
            row_scales(dve, link, r)
            for n in range(W8):
                k, c = n // 4, n % 4
                dve.wait_ge(u_ready, n + 1)
                w = wt[:, (k * 4 + c) * D:(k * 4 + c + 1) * D]
                dve.scalar_tensor_tensor(out=w, in0=psU[n % 2][:, 0:D], scalar=0.5, in1=w, op0=ALU.mult,
                                         op1=ALU.add).then_inc(u_free, 1)
            dve.wait_ge(u_free, 2 + W8)
            dve.sem_inc(w_ready, 1)

            def head_max(n, h):
                for qt in range(TPB):
                    dve.wait_ge(u_ready, n + h * 4 + qt + 1)
                    dve.tensor_reduce(mx[:, ds(h * 4 + qt, 1)], psU[qt % 2][:, :], AX, ALU.max).then_inc(u_free, 1)

            def normalise(i, g):
                dve.wait_ge(t_ready, turns(i) + 2 * (i + 1 < B) + g + 1)
                o = psT[:, :].rearrange("p (t a c) -> p t a c", t=TPB, c=32)
                rc = rec[:, :].rearrange("p (t a) -> p t a", t=TPB)
                dve.reciprocal(rc, o[:, :, :, HD]).then_inc(o_read, 1)
                dve.wait_ge(o_read, (i - 1) * 4 + g + 1)
                ao = AO[:, :].rearrange("p (t f) -> p t f", t=TPB)[:, :, ds(g * HPG * HD, HPG * HD)]
                dve.tensor_tensor(ao.rearrange("p t (a d) -> p t a d", d=HD), o[:, :, :, 0:HD],
                                  rc.unsqueeze(3).to_broadcast([P, TPB, HPG, HD]), ALU.mult).then_inc(t_free, 1)

            for i in range(-1, B + 1):
                s, n = i + 1, W8 + units(i)
                if s < B:
                    if s >= 1:
                        dve.wait_ge(t_ready, turns(i - 1) + 2)
                    layernorm(dve, r, s, xn, xn_ready)
                    for c in range(4):
                        dve.wait_ge(u_ready, n + c + 1)
                        dve.wait_ge(qf_free, 4 * s + c - 1 if 4 * s + c >= 2 else 0)
                        out = qf[:, (c % 2) * L:(c % 2 + 1) * L]
                        dve.tensor_scalar(out, psU[c % 2][:, :], bias_qk[:, c:c + 1], HD ** -0.5 if c < 2 else 1.0,
                                          ALU.add, ALU.mult).then_inc(u_free, 1)
                        dve.wait_ge(u_free, 2 + n + c + 1)
                        dve.sem_inc(qf_ready, 1)
                    if s == 0:
                        dve.wait_ge(ones_set, 1)
                    if s >= 3:
                        dve.wait_ge(v_staged, 4 * (s - 2))
                    for j in range(TPB):
                        dve.wait_ge(u_ready, n + 4 + j + 1)
                        o = ((s % 3) * TPB + j) * H * 32
                        dve.tensor_tensor(V[:, o:o + H * 32].rearrange("p (h c) -> p h c", c=32)[:, :, 0:HD],
                                          psU[j % 2][:, 0:D].rearrange("p (h c) -> p h c", c=HD),
                                          bias_v.rearrange("p (h c) -> p h c", c=HD), ALU.add).then_inc(u_free, 1)
                    dve.wait_ge(u_free, 2 + n + 8)
                    dve.sem_inc(v_ready, 1)
                    n += 8
                if 0 <= i:
                    with dve.Fori(0, NG) as g:
                        for c in range(HPG):
                            if i < B:
                                head_max(n, g * HPG + c)
                        if i >= 1:
                            normalise(i, g)
                    if i < B:
                        n += 64
                        dve.wait_ge(u_free, 2 + n)
                        dve.sem_inc(max_found, 1)
                if i >= 1:
                    dve.wait_ge(biased, 4 * i)
                    for j in range(TPB):
                        dve.wait_ge(u_ready, n + j + 1)
                        xj = x[:, ((i - 1) * TPB + j) * D:((i - 1) * TPB + j + 1) * D]
                        dve.tensor_tensor(xj, psU[j % 2][:, 0:D], xj, ALU.add).then_inc(u_free, 1)
                    dve.wait_ge(u_free, 2 + n + 4)
                    row_stats(dve, r, i - 1)

        @block.tensor
        def _(pe):
            def unit(n):
                pe.wait_ge(u_free, n + 1)

            for n in range(W8):
                k, c = n // 4, n % 4
                unit(n)
                pe.matmul(psU[n % 2][:, 0:D], lora_b[:, c * D + k * P:c * D + (k + 1) * P], lora_a[:, c * D:(c + 1) * D],
                          start=True, stop=True).then_inc(u_ready, 1)
            pe.wait_ge(w_ready, 1)
            w = lambda k, c, a, b: wt[:, (k * 4 + c) * D + a:(k * 4 + c) * D + b]

            def score_max(i, n, h):
                o = (i % 3) * SLOT
                for qt in range(TPB):
                    unit(n + h * 4 + qt)
                    pe.matmul(psU[qt % 2][:, :], QS[0:NT, ds(h * L + (o + qt * P), P)], KS[0:NT, ds(h * L + o, L)],
                              start=True, stop=True).then_inc(u_ready, 1)

            def scores(i, g, kt):
                st, o = (i - 1) * 16 + g * 4 + kt, ((i - 1) % 3) * SLOT
                for u in range(2):
                    pe.wait_ge(exp_done, 2 * st + u + 1)
                    for c in range(2):
                        h = g * HPG + (2 * u + c)
                        ins = pe.matmul(psS[u][:, c * L:(c + 1) * L], KS[0:KC, ds(h * L + (o + kt * P), P)],
                                        QS[0:KC, ds(h * L + o, L)], start=True, stop=True)
                    ins.then_inc(scored, 1)

            def values(i, g, kt):
                st = (i - 1) * 16 + g * 4 + kt
                if kt == 0:
                    pe.wait_ge(v_staged, (i - 1) * 4 + g + 1)
                    pe.wait_ge(o_copied, 1 + (i - 1) * 4 + g)
                pe.wait_ge(exp_done, 2 + 2 * st + 2)
                for c in range(HPG):
                    ins = pe.matmul(psO[32 * c:32 * c + 32, :], VG[:, (kt * HPG + c) * 32:(kt * HPG + c + 1) * 32],
                                    Pr[:, ((kt % 2) * 4 + c) * L:((kt % 2) * 4 + c + 1) * L],
                                    start=(kt == 0), stop=(kt == TPB - 1), tile_position=(0, 32 * c),
                                    skip_group_check=True)
                ins.then_inc(pv_done, 1)

            def turn_output(i, g):
                pe.wait_ge(o_copied, 1 + (i - 1) * 4 + g + 1)
                pe.wait_ge(t_free, turns(i) + 2 * (i + 1 < B) + g + 1)
                for t in range(TPB):
                    ins = pe.transpose(psT[:, t * P:(t + 1) * P], Osb[:, t * P:(t + 1) * P], ident[:, :])
                ins.then_inc(t_ready, 1)

            pe.sem_inc(pv_done, 2)
            for i in range(-1, B + 1):
                s, n, t = i + 1, W8 + units(i), turns(i)
                if s < B:
                    pe.wait_ge(xn_ready, 4 * s + 4)
                    for k in range(KD):
                        pe.wait_ge(t_free, t + k + 1)
                        for j in range(TPB):
                            ins = pe.transpose(psT[:, j * P:(j + 1) * P], xn[:, j * D + k * P:j * D + (k + 1) * P], ident[:, :])
                        ins.then_inc(t_ready, 1)
                    t += 2
                    pe.wait_ge(t_free, 1 + t)
                    for c in range(4):
                        unit(n + c)
                        for k in range(KD):
                            ins = pe.matmul(psU[c % 2][:, :], w(k, c // 2, (c % 2) * P, (c % 2 + 1) * P),
                                            xT[:, k * L:(k + 1) * L], start=(k == 0), stop=(k == KD - 1))
                        ins.then_inc(u_ready, 1)
                    for j in range(TPB):
                        unit(n + 4 + j)
                        for k in range(KD):
                            ins = pe.matmul(psU[j % 2][:, 0:D], xT[:, k * L + j * P:k * L + (j + 1) * P], w(k, 2, 0, D),
                                            start=(k == 0), stop=(k == KD - 1))
                        ins.then_inc(u_ready, 1)
                    n += 8
                if i == 0:
                    pe.wait_ge(ones_set, 1)
                if 0 <= i < B:
                    pe.wait_ge(terms_in, 16 * 12 * (i + 1))
                if i >= 1:
                    pe.wait_ge(max_in, 16 * i)
                if i >= 0:
                    with pe.Fori(0, NG) as g:
                        hi, lo = i < B, i >= 1
                        if lo:
                            scores(i, g, 0)
                        if hi:
                            score_max(i, n, g * HPG)
                        if lo:
                            scores(i, g, 1)
                            values(i, g, 0)
                        if hi:
                            score_max(i, n, g * HPG + 1)
                        if lo:
                            scores(i, g, 2)
                            values(i, g, 1)
                            scores(i, g, 3)
                            values(i, g, 2)
                        if hi:
                            score_max(i, n, g * HPG + 2)
                        if lo:
                            values(i, g, 3)
                        if hi:
                            score_max(i, n, g * HPG + 3)
                        if lo:
                            turn_output(i, g)
                if i >= 1:
                    t += 4
                if 0 <= i < B:
                    n += 64
                    pe.wait_ge(max_found, i + 1)
                    pe.wait_ge(t_free, t + 1)
                    pe.transpose(psT[0:64, 0:P], mx[:, :], ident[:, :]).then_inc(t_ready, 1)
                    t += 1
                if i >= 1:
                    for k in range(KD):
                        pe.wait_ge(t_free, t + k + 1)
                        for j in range(TPB):
                            ins = pe.transpose(psT[:, j * P:(j + 1) * P], AO[:, j * D + k * P:j * D + (k + 1) * P], ident[:, :])
                        ins.then_inc(t_ready, 1)
                    pe.wait_ge(t_free, 1 + t + 2)
                    for j in range(TPB):
                        unit(n + j)
                        for k in range(KD):
                            ins = pe.matmul(psU[j % 2][:, 0:D], AOT[:, k * L + j * P:k * L + (j + 1) * P], w(k, 3, 0, D),
                                            start=(k == 0), stop=(k == KD - 1))
                        ins.then_inc(u_ready, 1)


NE, TOPK, INTER = 32, 4, 128
NC = TILES * TOPK
NBLK = 96
assert NBLK >= B * L * TOPK // P + NE - 1


def routing_stage(nc, idx, iota, upper, token, slot, block_expert, slot_token, table_dram, spread):
    with ExitStack() as ctx:
        def sb(n, shape, dt=F32):
            return ctx.enter_context(nc.sbuf_tensor(f"rt_{n}", shape, dt))

        sems = []

        def sem(n):
            sems.append(ctx.enter_context(nc.semaphore(f"rt_{n}")))
            return sems[-1]

        W = NE * NC
        idxf, one, hot, upb, oneb = sb("idxf", [P, NC]), sb("one", [P, 1]), sb("hot", [P, W], BF16), sb("upb", [P, P], BF16), sb("oneb", [P, P], BF16)
        run, val = sb("run", [P, W]), sb("val", [P, W])
        start, cnt, nbf, bend, off = (sb(n, [P, NE]) for n in ("start", "cnt", "nbf", "bend", "off"))
        cnti = sb("cnti", [P, NE], I32)
        slotf, lof, hif = (sb(n, [P, NC]) for n in ("slotf", "lof", "hif"))
        lo, hi, place = (sb(n, [P, NC], I32) for n in ("lo", "hi", "place"))
        cmp, bexp, zero = sb("cmp", [1, NBLK * NE]), sb("bexp", [1, NBLK]), sb("zero", [P, NBLK], I32)
        psW = ctx.enter_context(nc.psum_tensor("rt_psW", [P, W], F32))
        psC = ctx.enter_context(nc.psum_tensor("rt_psC", [P, W], F32))
        dstep, hot_ready, counted, zero_ready, zeroed, placed, table_in = (sem(n) for n in (
            "dstep", "hot_ready", "counted", "zero_ready", "zeroed", "placed", "table_in"))
        clear_after(ctx, nc, sems)
        block = ctx.enter_context(nc.Block())

        @block.vector
        def _(dve):
            link = Link(dve, dstep)
            dve.memset(zero[:, :], 0).then_inc(zero_ready, 1)
            link(dve.tensor_copy(idxf[:, :], idx[:, :]))
            dve.memset(oneb[:, :], 1.0)
            dve.memset(one[:, :], 1.0)
            dve.tensor_copy(upb[:, :], upper[:, :])
            ec = lambda t: t[:, :].rearrange("p (e c) -> p e c", c=NC)
            dve.tensor_tensor(ec(hot), idxf[:, :].unsqueeze(1).to_broadcast([P, NE, NC]),
                              iota[:, 0:NE].unsqueeze(2).to_broadcast([P, NE, NC]), ALU.is_equal).then_inc(hot_ready, 1)
            dve.wait_ge(counted, 1)
            link(dve.tensor_tensor_scan(run[:, :], one[:, 0:1].to_broadcast([P, W]), psC[:, :], 0.0, ALU.mult, ALU.add))
            dve.memset(start[:, 0:1], 0.0)
            link(dve.tensor_copy(start[:, 1:NE], ec(run)[:, 0:NE - 1, NC - 1]))
            link(dve.tensor_tensor(cnt[:, :], ec(run)[:, :, NC - 1], start[:, :], ALU.subtract))
            link(dve.tensor_scalar(cnti[:, :], cnt[:, :], float(P - 1), None, ALU.add))
            link(dve.tensor_scalar(cnti[:, :], cnti[:, :], 7, None, ALU.logical_shift_right))
            link(dve.tensor_copy(nbf[:, :], cnti[:, :]))
            link(dve.tensor_tensor_scan(bend[:, :], one[:, 0:1].to_broadcast([P, NE]), nbf[:, :], 0.0, ALU.mult, ALU.add))
            link(dve.tensor_tensor(off[:, :], bend[:, :], nbf[:, :], ALU.subtract))
            link(dve.scalar_tensor_tensor(out=off[:, :], in0=off[:, :], scalar=float(P), in1=start[:, :], op0=ALU.mult,
                                          op1=ALU.subtract))
            link(dve.tensor_tensor(val[:, :], run[:, :], psC[:, :], ALU.subtract))
            link(dve.tensor_tensor(val[:, :], psW[:, :], val[:, :], ALU.add))
            link(dve.tensor_tensor(ec(val), ec(val), off[:, :].unsqueeze(2).to_broadcast([P, NE, NC]), ALU.add))
            link(dve.tensor_tensor(val[:, :], val[:, :], hot[:, :], ALU.mult))
            link(dve.tensor_reduce(slotf[:, :], val[:, :].rearrange("p (e c) -> p c e", c=NC), AX, ALU.add))
            link(dve.tensor_copy(slot[:, :], slotf[:, :]))
            link(dve.tensor_scalar(lo[:, :], slot[:, :], P - 1, None, ALU.bitwise_and))
            link(dve.tensor_scalar(hi[:, :], slot[:, :], 7, None, ALU.logical_shift_right))
            link(dve.tensor_copy(lof[:, :], lo[:, :]))
            link(dve.tensor_copy(hif[:, :], hi[:, :]))
            dve.scalar_tensor_tensor(out=place[:, :], in0=lof[:, :], scalar=float(NBLK), in1=hif[:, :], op0=ALU.mult,
                                     op1=ALU.add).then_inc(placed, 1)
            c3 = cmp[:, :].rearrange("p (n e) -> p n e", e=NE)
            link(dve.tensor_tensor(c3, bend[0:1, :].unsqueeze(1).to_broadcast([1, NBLK, NE]),
                                   iota[0:1, 0:NBLK].unsqueeze(2).to_broadcast([1, NBLK, NE]), ALU.is_le))
            link(dve.tensor_reduce(bexp[:, :], c3, AX, ALU.add))
            link(dve.tensor_scalar(block_expert[:, :], bexp[:, :], float(NE - 1), None, ALU.min))

        @block.tensor
        def _(pe):
            pe.wait_ge(hot_ready, 1)
            for q in range(W // 512):
                c = slice(q * 512, (q + 1) * 512)
                pe.matmul(psC[:, c], oneb[:, :], hot[:, c], start=True, stop=True)
                ins = pe.matmul(psW[:, c], upb[:, :], hot[:, c], start=True, stop=True)
            ins.then_inc(counted, 1)

        @block.sync
        def _(sp):
            sp.wait_ge(zero_ready, 1)
            sp.dma_start(table_dram.rearrange("(p n) o -> p (n o)", p=P), zero[:, :]).then_inc(zeroed, 16)
            sp.wait_ge(spread, 16 * NC)
            sp.dma_start(slot_token[:, :], table_dram.rearrange("(p n) o -> p (n o)", p=P)).then_inc(table_in, 16)
            sp.wait_ge(table_in, 16)

        @block.gpsimd
        def _(pool):
            pool.wait_ge(placed, 1)
            pool.wait_ge(zeroed, 16)
            for c in range(NC):
                pool.indirect_dma_start(out=table_dram, out_offset=bass.IndirectOffsetOnAxis(ap=place[:, c:c + 1], axis=0),
                                        in_=token[:, c:c + 1], in_offset=None).then_inc(spread, 16)


def moe_stage(nc, tag, r, ident, weights, weights_in, slot, half_weight, block_expert, slot_token, rows_dram, out_dram):
    x = r.x
    GU, DW = weights[:, 0:NE * KD * 2 * INTER], weights[:, NE * KD * 2 * INTER:]
    NG = 4
    with ExitStack() as ctx:
        def sb(n, shape, dt=F32):
            return ctx.enter_context(nc.sbuf_tensor(f"{tag}_{n}", shape, dt))

        def ps(n):
            return [ctx.enter_context(nc.psum_tensor(f"{tag}_{n}{i}", [P, 512], F32)) for i in range(2)]

        def sem(n):
            return ctx.enter_context(nc.semaphore(f"{tag}_{n}"))

        xn = sb("xn", [P, 2 * TPB * D])
        xg = sb("xg", [P, NG * D])
        xgT, sg, hm, hT, ys = sb("xgT", [P, 2 * D]), sb("sg", [P, 2 * P]), sb("hm", [P, 2 * P]), sb("hT", [P, 2 * P]), sb("ys", [P, 4 * D])
        psX, psG, psH, psY = ps("psX"), ps("psG"), ps("psH"), ps("psY")
        dstep, xn_ready, turned, xT_ready, gu_done, sg_ready, hm_ready, h_turned, hT_ready, y_done, y_copied = (
            sem(n) for n in ("dstep", "xn_ready", "turned", "xT_ready", "gu_done", "sg_ready", "hm_ready",
                             "h_turned", "hT_ready", "y_done", "y_copied"))
        gathered = [sem(f"gathered{i}") for i in range(NG)]
        saved = [sem(f"saved{i}") for i in range(4)]
        stored = [sem(f"stored{i}") for i in range(2)]
        picked = [sem(f"picked{i}") for i in range(NG)]
        added, at_ready, ptick = sem("added"), sem("at_ready"), sem("ptick")
        at = sb("at", [P, 4], I32)
        block = ctx.enter_context(nc.Block())

        def blocks(eng, steps, lead, lag):
            lo, hi = -lead, NBLK + lag
            first = 4 * -(-lag // 4)
            last = first + 4 * ((NBLK - lead - first) // 4)
            for b in range(lo, first):
                steps(b, b % 4, {})
            with eng.Fori(first // 4, last // 4) as q:
                known = {}
                for j in range(4):
                    steps(q * 4 + j, j, known)
            for b in range(last, hi):
                steps(b, b % 4, {})

        def inside(b):
            return not isinstance(b, int) or 0 <= b < NBLK

        @block.sync
        def _(sp):
            for s in range(B):
                sp.wait_ge(xn_ready, TPB * (s + 1))
                o = (s % 2) * TPB * D
                sp.dma_start(rows_dram[s * L:(s + 1) * L, :].rearrange("(t p) d -> p t d", p=P),
                             xn[:, o:o + TPB * D].rearrange("p (t d) -> p t d", d=D)).then_inc(stored[s % 2], 16)

            def save(b, j, known):
                sp.wait_ge(y_copied, b + 1)
                sp.dma_start(out_dram[ds(b * P, P), :], ys[:, j * D:(j + 1) * D]).then_inc(saved[j], 16)

            blocks(sp, save, 0, 0)

        @block.gpsimd
        def _(pool):
            for st in stored:
                pool.wait_ge(st, 16 * B // 2)

            def gather(b, j, known):
                if not isinstance(b, int) or b >= 4:
                    pool.wait_ge(turned, b - 3)
                stand(pool, ptick)
                pool.tensor_copy(at[:, j:j + 1], slot_token[:, ds(b, 1)]).then_inc(at_ready, 1)
                pool.wait_ge(at_ready, b + 1)
                stand(pool, ptick)
                pool.indirect_dma_start(out=xg[:, j * D:(j + 1) * D], out_offset=None, in_=rows_dram,
                                        in_offset=bass.IndirectOffsetOnAxis(ap=at[:, j:j + 1], axis=0)
                                        ).then_inc(gathered[j], 16)

            for b in range(4):
                gather(b, b, {})
            with pool.Fori(1, NBLK // 4) as q:
                for j in range(4):
                    gather(q * 4 + j, j, {})
            for j in range(4):
                pool.wait_ge(saved[j], 16 * NBLK // 4)
            pool.wait_ge(turned, NBLK)

            def pick(c, j):
                stand(pool, ptick)
                pool.tensor_copy(at[:, j:j + 1], slot[:, ds(c, 1)]).then_inc(at_ready, 1)
                pool.wait_ge(at_ready, NBLK + c + 1)
                stand(pool, ptick)
                pool.indirect_dma_start(out=xg[:, j * D:(j + 1) * D], out_offset=None, in_=out_dram,
                                        in_offset=bass.IndirectOffsetOnAxis(ap=at[:, j:j + 1], axis=0)
                                        ).then_inc(picked[j], 16)

            for c in range(4):
                pick(c, c)
            with pool.Fori(1, NC // 4) as q:
                for j in range(4):
                    pool.wait_ge(added, q * 4 + (j - 3))
                    pick(q * 4 + j, j)

        @block.scalar
        def _(act):
            def steps(b, j, known):
                if inside(b):
                    act.wait_ge(turned, b + 1)
                    if not isinstance(b, int) or b >= 2:
                        act.wait_ge(gu_done, b - 1)
                    act.copy(xgT[:, (j % 2) * D:(j % 2 + 1) * D], psX[j % 2][:, 0:D]).then_inc(xT_ready, 1)
                m, jm = (b - 1), (j - 1) % 4
                if inside(m):
                    act.wait_ge(gu_done, m + 1)
                    if not isinstance(m, int) or m >= 2:
                        act.wait_ge(hm_ready, m - 1)
                    act.activation(sg[:, (jm % 2) * P:(jm % 2 + 1) * P], psG[jm % 2][:, 0:P], ACT.Silu).then_inc(sg_ready, 1)
                m, jm = (b - 3), (j - 3) % 4
                if inside(m):
                    act.wait_ge(y_done, m + 1)
                    if not isinstance(m, int) or m >= 4:
                        act.wait_ge(saved[jm], (m - jm) * 4)
                    act.copy(ys[:, jm * D:(jm + 1) * D], psY[jm % 2][:, 0:D]).then_inc(y_copied, 1)

            blocks(act, steps, 0, 3)

        @block.vector
        def _(dve):
            link = Link(dve, dstep)
            row_scales(dve, link, r)
            for s in range(B):
                if s >= 2:
                    dve.wait_ge(stored[s % 2], 16)
                o = (s % 2) * TPB * D
                layernorm(dve, r, s, xn[:, o:o + TPB * D], xn_ready)

            def steps(b, j, known):
                if inside(b):
                    dve.wait_ge(sg_ready, b + 1)
                    if not isinstance(b, int) or b >= 2:
                        dve.wait_ge(h_turned, b - 1)
                    dve.tensor_tensor(hm[:, (j % 2) * P:(j % 2 + 1) * P], psG[j % 2][:, P:2 * P],
                                      sg[:, (j % 2) * P:(j % 2 + 1) * P], ALU.mult).then_inc(hm_ready, 1)
                m, jm = b - 1, (j - 1) % 4
                if inside(m):
                    dve.wait_ge(h_turned, m + 1)
                    if not isinstance(m, int) or m >= 2:
                        dve.wait_ge(y_done, m - 1)
                    dve.tensor_copy(hT[:, (jm % 2) * P:(jm % 2 + 1) * P], psH[jm % 2][:, 0:P]).then_inc(hT_ready, 1)

            blocks(dve, steps, 0, 1)

            def add(t):
                for j in range(TOPK):
                    dve.wait_ge(picked[j], (t + 1) * 16)
                    if j or not isinstance(t, int):
                        dve.wait_ge(added, t * TOPK + j)
                    xt = x[:, ds(t * D, D)]
                    dve.scalar_tensor_tensor(out=xt, in0=xg[:, j * D:(j + 1) * D], scalar=half_weight[:, ds(t * TOPK + j, 1)],
                                             in1=xt, op0=ALU.mult, op1=ALU.add).then_inc(added, 1)
                dve.wait_ge(added, (t + 1) * TOPK)
                dve.bn_stats(r.stats[:, ds(6 * t, 6)], x[:, ds(t * D, D)])

            add(0)
            with dve.Fori(1, TILES) as t:
                add(t)

        @block.tensor
        def _(pe):
            for q in range(weights_in[1]):
                pass
            pe.wait_ge(weights_in[0], weights_in[1])

            def steps(b, j, known):
                m, jm = b + 1, (j + 1) % 4
                if inside(m):
                    pe.wait_ge(gathered[jm], (m - jm) * 4 + 16)
                    if not isinstance(m, int) or m >= 2:
                        pe.wait_ge(xT_ready, m - 1)
                    for k in range(KD):
                        ins = pe.transpose(psX[jm % 2][:, k * P:(k + 1) * P], xg[:, jm * D + k * P:jm * D + (k + 1) * P],
                                           ident[:, :])
                    ins.then_inc(turned, 1)

                def expert(m, jm):
                    if jm not in known:
                        known[jm] = pe.value_load(block_expert[0:1, ds(m, 1)], min_val=0, max_val=NE - 1)
                    return known[jm]

                if inside(b):
                    e = expert(b, j)
                    pe.wait_ge(xT_ready, b + 1)
                    if not isinstance(b, int) or b >= 2:
                        pe.wait_ge(hm_ready, b - 1)
                    for k in range(KD):
                        ins = pe.matmul(psG[j % 2][:, 0:2 * INTER], xgT[:, (j % 2) * D + k * P:(j % 2) * D + (k + 1) * P],
                                        GU[:, ds(e * (KD * 2 * INTER) + k * 2 * INTER, 2 * INTER)],
                                        start=(k == 0), stop=(k == KD - 1))
                    ins.then_inc(gu_done, 1)
                m, jm = b - 1, (j - 1) % 4
                if inside(m):
                    pe.wait_ge(hm_ready, m + 1)
                    if not isinstance(m, int) or m >= 2:
                        pe.wait_ge(hT_ready, m - 1)
                    pe.transpose(psH[jm % 2][:, 0:P], hm[:, (jm % 2) * P:(jm % 2 + 1) * P], ident[:, :]).then_inc(h_turned, 1)
                m, jm = b - 2, (j - 2) % 4
                if inside(m):
                    e = known.pop(jm) if jm in known and j >= 2 else expert(m, jm)
                    if j < 2:
                        known.pop(jm)
                    pe.wait_ge(hT_ready, m + 1)
                    if not isinstance(m, int) or m >= 2:
                        pe.wait_ge(y_copied, m - 1)
                    pe.matmul(psY[jm % 2][:, 0:D], hT[:, (jm % 2) * P:(jm % 2 + 1) * P], DW[:, ds(e * D, D)],
                              start=True, stop=True).then_inc(y_done, 1)

            blocks(pe, steps, 1, 2)


H1, DN, DR, DV, QR, KVR = 16, 128, 64, 128, 96, 64
ND = QR + KVR + DR
PAIRS = H1 // 2


class Latent:

    def __init__(self, ctx, nc):
        def sb(n, shape, dt=F32):
            return ctx.enter_context(nc.sbuf_tensor(f"la_{n}", shape, dt))

        self.down, self.norm = sb("down", [P, KD * ND]), sb("norm", [P, QR + KVR])
        self.qw, self.qsw = sb("qw", [QR, H1 * P]), sb("qsw", [QR, PAIRS * P])
        self.vo = sb("vo", [P, PAIRS * D])
        self.cos, self.sin = sb("cos", [P, 2 * L]), sb("sin", [P, L])
        self.kcos, self.ksin = sb("kcos", [P, P]), sb("ksin", [P, P])
        self.maskf, self.mask, self.identb = sb("maskf", [P, P]), sb("mask", [P, P], BF16), sb("identb", [P, P], BF16)


def latent_weights(nc, la, ident, qup, kup, vup, wo, loads, loaded):
    with ExitStack() as ctx:
        ps = [ctx.enter_context(nc.psum_tensor(f"lw_ps{i}", [P, 512], F32)) for i in range(4)]
        made, kept = ctx.enter_context(nc.semaphore("lw_made")), ctx.enter_context(nc.semaphore("lw_kept"))
        block = ctx.enter_context(nc.Block())

        @block.sync
        def _(sp):
            for dst, src in loads:
                sp.dma_start(dst, src).then_inc(loaded, 16)

        @block.tensor
        def _(pe):
            pe.wait_ge(loaded, 16 * len(loads))
            for h in range(H1):
                pe.wait_ge(kept, max(h - 3, 0))
                pe.matmul(ps[h % 4][0:QR, 0:KVR], qup[:, h * QR:(h + 1) * QR], kup[:, h * KVR:(h + 1) * KVR],
                          start=True, stop=True).then_inc(made, 1)
            for c in range(PAIRS):
                pe.wait_ge(kept, H1 + c - 3)
                for e in range(2):
                    h = 2 * c + e
                    ins = pe.matmul(ps[c % 4][64 * e:64 * e + 64, 0:D], vup[:, h * KVR:(h + 1) * KVR],
                                    wo[:, h * D:(h + 1) * D], start=True, stop=True, tile_position=(0, 64 * e))
                ins.then_inc(made, 1)

        @block.vector
        def _(dve):
            dve.wait_ge(loaded, 16 * len(loads))
            for h in range(H1):
                dve.wait_ge(made, h + 1)
                o = h * P + (DR if h % 2 == 0 else 0)
                dve.tensor_copy(la.qw[:, o:o + KVR], ps[h % 4][0:QR, 0:KVR]).then_inc(kept, 1)
            for c in range(PAIRS):
                dve.wait_ge(made, H1 + c + 1)
                dve.tensor_copy(la.vo[:, c * D:(c + 1) * D], ps[c % 4][:, 0:D]).then_inc(kept, 1)
            dve.tensor_copy(la.identb[:, :], ident[:, :])
            dve.tensor_copy(la.mask[:, :], la.maskf[:, :])


def latent_stage(nc, r, ident, la):
    SC = float(1.0 / np.sqrt(np.float32(DN + DR)))
    AT = {3: 0, 2: 512, 0: 896, 1: 1024}
    BT = {0: 0, 1: 512, 3: 896, 2: 1024}
    NS = 1280
    U_X, U_D, U_Q, U_K = 0, 2, 6, 7
    U_P = 9
    NU = U_P + 3 * PAIRS
    x = r.x
    with ExitStack() as ctx:
        def sb(n, shape, dt=F32):
            return ctx.enter_context(nc.sbuf_tensor(f"a1_{n}", shape, dt))

        def sem(n):
            return ctx.enter_context(nc.semaphore(f"a1_{n}"))

        oT, qT = sb("oT", [P, PAIRS * L]), sb("qT", [QR, L])
        xn, xT, dn, qn = oT[:, 0:1024], oT[:, 1024:2048], oT[:, 2048:2048 + TPB * ND], oT[:, 2944:2944 + TPB * QR]
        kn, kT = sb("kn", [P, TPB * 192]), sb("kT", [P, 2 * L])
        ss, sv, sr, st, junk = sb("ss", [P, 8]), sb("sv", [P, 8]), sb("sr", [P, 8]), sb("st", [P, 8]), sb("junk", [P, QR])
        ra, rb = sb("ra", [P, P]), sb("rb", [P, P])
        q = [sb(f"q{i}", [P, L]) for i in range(4)]
        t2 = sb("t2", [P, 2 * L])
        mx, nb, sums, rec = sb("mx", [P, 4]), sb("nb", [P, 4]), sb("sums", [P, 4]), sb("rec", [P, 4])
        pr, prT = [sb(f"pr{i}", [P, NS]) for i in range(2)], [sb(f"prT{i}", [P, NS]) for i in range(2)]
        psA = ctx.enter_context(nc.psum_tensor("a1_psA", [P, 1536], F32))
        psP = ctx.enter_context(nc.psum_tensor("a1_psP", [P, 1536], F32))
        psU = ctx.enter_context(nc.psum_tensor("a1_psU", [P, 512], F32))
        psO = ctx.enter_context(nc.psum_tensor("a1_psO", [P, 512], F32))
        (dstep, pstep, u_ready, u_free, xn_ready, ss_ready, kv_ready, kn_ready, q_part, q_ready, a_done, nb_ready,
         exp_done, quotient, turned, pT_ready, v_done, o_copied, out_done, added, ptick) = (sem(n) for n in (
             "dstep", "pstep", "u_ready", "u_free", "xn_ready", "ss_ready", "kv_ready", "kn_ready", "q_part", "q_ready",
             "a_done", "nb_ready", "exp_done", "quotient", "turned", "pT_ready", "v_done", "o_copied", "out_done",
             "added", "ptick"))
        block = ctx.enter_context(nc.Block())

        @block.tensor
        def _(pe):
            pe.sem_inc(v_done, 1)
            pe.sem_inc(turned, 2)
            pe.sem_inc(out_done, 1)
            with pe.Fori(0, B) as b:
                def unit(n):
                    pe.wait_ge(u_free, 1 + b * NU + n)

                pe.wait_ge(xn_ready, b * TPB + TPB)
                for k in range(KD):
                    unit(U_X + k)
                    for j in range(TPB):
                        ins = pe.transpose(psU[:, j * P:(j + 1) * P], xn[:, j * D + k * P:j * D + (k + 1) * P], ident[:, :])
                    ins.then_inc(u_ready, 1)
                for j in range(TPB):
                    unit(U_D + j)
                    for k in range(KD):
                        ins = pe.matmul(psU[:, 0:ND], xT[:, k * L + j * P:k * L + (j + 1) * P], la.down[:, k * ND:(k + 1) * ND],
                                        start=(k == 0), stop=(k == KD - 1))
                    ins.then_inc(u_ready, 1)
                unit(U_Q)
                pe.wait_ge(kv_ready, b + 1)
                for j in range(TPB):
                    ins = pe.transpose(psU[0:QR, j * P:(j + 1) * P], qn[:, j * QR:(j + 1) * QR], ident[:, :])
                ins.then_inc(u_ready, 1)
                pe.wait_ge(kn_ready, b + 1)
                for e in range(2):
                    unit(U_K + e)
                    o = 64 if e == 0 else 0
                    for j in range(TPB):
                        ins = pe.transpose(psU[:, j * P:(j + 1) * P], kn[:, j * 192 + o:j * 192 + o + P], ident[:, :])
                    ins.then_inc(u_ready, 1)

                def queries(c, part):
                    unit(U_P + 3 * c + part)
                    w = la.qsw[:, c * P:(c + 1) * P] if part == 1 else la.qw[:, (2 * c + part // 2) * P:(2 * c + part // 2 + 1) * P]
                    pe.matmul(psU[:, :], w, qT[:, :], start=True, stop=True).then_inc(u_ready, 1)

                def scores(h):
                    pe.wait_ge(q_ready, b * H1 + h + 1)
                    pe.wait_ge(exp_done, 1 + b * H1 + h)
                    qh, kh = q[h % 4], kT[:, (h % 2) * L:(h % 2 + 1) * L]
                    for t in (3, 2, 0, 1):
                        pe.matmul(psA[:, AT[t]:AT[t] + (t + 1) * P], qh[:, t * P:(t + 1) * P], kh[:, 0:(t + 1) * P],
                                  start=True, stop=False)
                        ins = pe.matmul(psA[:, AT[t] + t * P:AT[t] + (t + 1) * P], la.identb[:, :], la.mask[:, :],
                                        start=False, stop=True)
                    ins.then_inc(a_done, 1)

                def turn(h):
                    pe.wait_ge(quotient, b * H1 + h + 1)
                    pe.wait_ge(pT_ready, 1 + b * H1 + h)
                    for kt in range(TPB):
                        for qt in range(kt, TPB):
                            ins = pe.transpose(psP[:, BT[kt] + (qt - kt) * P:BT[kt] + (qt - kt + 1) * P],
                                               pr[h % 2][:, AT[qt] + kt * P:AT[qt] + (kt + 1) * P], ident[:, :])
                    ins.then_inc(turned, 1)

                def values(c):
                    pe.wait_ge(pT_ready, 1 + b * H1 + 2 * c + 2)
                    pe.wait_ge(o_copied, 1 + b * PAIRS + c)
                    for t in range(TPB):
                        for e in range(2):
                            ins = pe.matmul(psO[64 * e:64 * e + 64, t * P:L], kn[:, t * 192:t * 192 + KVR],
                                            prT[e][:, BT[t]:BT[t] + L - t * P], start=(t == 0), stop=(t == TPB - 1),
                                            tile_position=(0, 64 * e), skip_group_check=True)
                    ins.then_inc(v_done, 1)

                pe.wait_ge(u_free, 1 + b * NU + U_P)
                for part in range(3):
                    queries(0, part)
                for s in range(H1 + 2):
                    if s < H1:
                        scores(s)
                    if s >= 3 and s % 2:
                        values((s - 3) // 2)
                    if s < H1 - 2:
                        for part in ((0, 1) if s % 2 == 0 else (2,)):
                            queries(s // 2 + 1, part)
                    if 1 <= s <= H1:
                        turn(s - 1)
                pe.wait_ge(o_copied, 1 + b * PAIRS + PAIRS)
                outs = [psA[:, 0:D], psA[:, 512:512 + D], psA[:, 1024:1024 + D], psP[:, 0:D]]
                for t in range(TPB):
                    for c in range(PAIRS):
                        ins = pe.matmul(outs[t], oT[:, c * L + t * P:c * L + (t + 1) * P], la.vo[:, c * D:(c + 1) * D],
                                        start=(c == 0), stop=(c == PAIRS - 1))
                ins.then_inc(out_done, 1)

        @block.scalar
        def _(act):
            act.sem_inc(exp_done, 1)
            act.sem_inc(o_copied, 1)
            act.sem_inc(pT_ready, 1)
            with act.Fori(0, B) as b:
                for j in range(TPB):
                    act.wait_ge(u_free, 1 + b * NU + U_D + j + 1)
                    for c, (lo, w) in enumerate(((0, QR), (QR, KVR))):
                        act.activation(junk[:, 0:w], dn[:, j * ND + lo:j * ND + lo + w], ACT.Square,
                                       accum_out=ss[:, 2 * j + c:2 * j + c + 1]).then_inc(ss_ready, 1)
                        act.wait_ge(ss_ready, b * 8 + 2 * j + c + 1)
                for s in range(H1 + 2):
                    if s < H1:
                        act.wait_ge(nb_ready, b * H1 + s + 1)
                        act.wait_ge(turned, b * H1 + s + 1)
                        for t in (3, 2, 0, 1):
                            ins = act.activation(pr[s % 2][:, AT[t]:AT[t] + (t + 1) * P], psA[:, AT[t]:AT[t] + (t + 1) * P],
                                                 ACT.Exp, bias=nb[:, t:t + 1], scale=SC, accum_out=sums[:, t:t + 1])
                        ins.then_inc(exp_done, 1)
                    if s >= 3 and s % 2:
                        c = (s - 3) // 2
                        act.wait_ge(v_done, 1 + b * PAIRS + c + 1)
                        if c == 0:
                            act.wait_ge(out_done, b + 1)
                        act.copy(oT[:, c * L:(c + 1) * L], psO[:, :]).then_inc(o_copied, 1)
                    if 1 <= s <= H1:
                        h = s - 1
                        act.wait_ge(turned, 2 + b * H1 + h + 1)
                        act.wait_ge(v_done, 1 + b * PAIRS + h // 2)
                        act.copy(prT[h % 2][:, :], psP[:, 0:NS]).then_inc(pT_ready, 1)

        @block.gpsimd
        def _(pool):
            step = Link(pool, pstep, ptick)
            K3 = lambda t, w, a, c: t.rearrange("p (j c) -> p j c", c=w)[:, :, a:a + c]
            NP = 6
            with pool.Fori(0, B) as b:
                step.body(b * NP)
                pool.wait_ge(kv_ready, b + 1)
                h = DR // 2
                x1, x2 = K3(dn, ND, QR + KVR, h), K3(dn, ND, QR + KVR + h, h)
                cs, sn = K3(la.kcos[:, :], h, 0, h), K3(la.ksin[:, :], h, 0, h)
                a3, b3, k3 = K3(ra[:, :], h, 0, h), K3(rb[:, :], h, 0, h), kn[:, :]
                step(pool.tensor_tensor(a3, x1, cs, ALU.mult))
                step(pool.tensor_tensor(b3, x2, sn, ALU.mult))
                step(pool.tensor_tensor(K3(k3, 192, 64, h), a3, b3, ALU.subtract))
                step(pool.tensor_tensor(a3, x1, sn, ALU.mult))
                step(pool.tensor_tensor(b3, x2, cs, ALU.mult))
                step(pool.tensor_tensor(K3(k3, 192, 64 + h, h), a3, b3, ALU.add))
                pool.tensor_copy(K3(k3, 192, 128, 64), K3(k3, 192, 0, 64)).then_inc(kn_ready, 1)
                pool.wait_ge(kn_ready, b + 1)
                assert step.n == NP, step.n
                for h in range(H1):
                    pool.wait_ge(q_part, b * H1 + h + 1)
                    qh, rows = q[h % 4], slice(64 * (h % 2), 64 * (h % 2) + 64)
                    pool.tensor_tensor(qh[rows, :], qh[rows, :], t2[rows, (h // 2 % 2) * L:(h // 2 % 2 + 1) * L],
                                       ALU.add).then_inc(q_ready, 1)
                    pool.wait_ge(q_ready, b * H1 + h + 1)

        @block.vector
        def _(dve):
            link = Link(dve, dstep)
            dve.sem_inc(u_free, 1)
            row_scales(dve, link, r)
            first = link.n
            NL = 13 + H1 * 2
            with dve.Fori(0, B) as b:
                link.body(first + b * NL)

                def ready(n):
                    dve.wait_ge(u_ready, b * NU + n + 1)

                layernorm(dve, r, b, xn, xn_ready)
                for k in range(KD):
                    ready(U_X + k)
                    dve.tensor_copy(xT[:, k * L:(k + 1) * L], psU[:, :]).then_inc(u_free, 1)
                for j in range(TPB):
                    ready(U_D + j)
                    dve.tensor_copy(dn[:, j * ND:(j + 1) * ND], psU[:, 0:ND]).then_inc(u_free, 1)
                dve.wait_ge(ss_ready, b * 8 + 8)
                two = lambda t, c: t[:, :].rearrange("p (j c) -> p j c", c=2)[:, :, c]
                dve.tensor_scalar(two(sv, 0), two(ss, 0), 1.0 / QR, 1e-6, ALU.mult, ALU.add)
                link(dve.tensor_scalar(two(sv, 1), two(ss, 1), 1.0 / KVR, 1e-6, ALU.mult, ALU.add))
                inverse_root(dve, link, sv[:, :], sr[:, :], st[:, :])
                for j in range(TPB):
                    dve.scalar_tensor_tensor(out=qn[:, j * QR:(j + 1) * QR], in0=dn[:, j * ND:j * ND + QR],
                                             scalar=sr[:, 2 * j:2 * j + 1], in1=la.norm[:, 0:QR], op0=ALU.mult, op1=ALU.mult)
                    ins = dve.scalar_tensor_tensor(out=kn[:, j * 192:j * 192 + KVR], in0=dn[:, j * ND + QR:j * ND + QR + KVR],
                                                   scalar=sr[:, 2 * j + 1:2 * j + 2], in1=la.norm[:, QR:QR + KVR],
                                                   op0=ALU.mult, op1=ALU.mult)
                ins.then_inc(kv_ready, 1)
                ready(U_Q)
                dve.tensor_copy(qT[:, :], psU[0:QR, :]).then_inc(u_free, 1)
                for e in range(2):
                    ready(U_K + e)
                    dve.tensor_copy(kT[:, e * L:(e + 1) * L], psU[:, :]).then_inc(u_free, 1)

                def queries(c, part):
                    n = U_P + 3 * c + part
                    ready(n)
                    if part == 1:
                        if c >= 2:
                            dve.wait_ge(q_ready, b * H1 + 2 * c - 2)
                        dve.tensor_tensor(t2[:, (c % 2) * L:(c % 2 + 1) * L], psU[:, :], la.sin[:, :],
                                          ALU.mult).then_inc(u_free, 1)
                        dve.wait_ge(u_free, 1 + b * NU + n + 1)
                        dve.sem_inc(q_part, 1)
                    else:
                        e = part // 2
                        if c >= 2:
                            dve.wait_ge(a_done, b * H1 + 2 * c + e - 3)
                        dve.tensor_tensor(q[(2 * c + e) % 4][:, :], psU[:, :], la.cos[:, e * L:(e + 1) * L],
                                          ALU.mult).then_inc(u_free, 1)
                        if e:
                            dve.wait_ge(u_free, 1 + b * NU + n + 1)
                            dve.sem_inc(q_part, 1)

                for part in range(3):
                    queries(0, part)
                for s in range(H1 + 1):
                    if s >= 1:
                        dve.wait_ge(exp_done, 1 + b * H1 + s)
                        link(dve.reciprocal(rec[:, :], sums[:, :]))
                        for t in (3, 2, 0, 1):
                            pt = pr[(s - 1) % 2][:, AT[t]:AT[t] + (t + 1) * P]
                            ins = dve.tensor_scalar(pt, pt, rec[:, t:t + 1], None, ALU.mult)
                        ins.then_inc(quotient, 1)
                    if s < H1:
                        dve.wait_ge(a_done, b * H1 + s + 1)
                        for t in (3, 2, 0, 1):
                            ins = dve.tensor_reduce(mx[:, t:t + 1], psA[:, AT[t]:AT[t] + (t + 1) * P], AX, ALU.max)
                        link(ins)
                        dve.tensor_scalar(nb[:, :], mx[:, :], -SC, None, ALU.mult).then_inc(nb_ready, 1)
                    if s < H1 - 2:
                        for part in ((0, 1) if s % 2 == 0 else (2,)):
                            queries(s // 2 + 1, part)
                dve.wait_ge(out_done, 1 + b + 1)
                for t, out in enumerate((psA[:, 0:D], psA[:, 512:512 + D], psA[:, 1024:1024 + D], psP[:, 0:D])):
                    xt = x[:, ds((b * TPB + t) * D, D)]
                    ins = dve.tensor_tensor(xt, out, xt, ALU.add)
                link(ins)
                row_stats(dve, r, b).then_inc(added, 1)
                assert link.n == NL, link.n


def latent_layout(a):
    g = lambda n: np.asarray(a["L1_attn_" + n])
    f = np.float32
    down = np.concatenate([g("wq_down"), g("wkv_down"), g("wk_rope")[:, 0::2], g("wk_rope")[:, 1::2]], 1)
    down = down.reshape(KD, P, ND).transpose(1, 0, 2).reshape(P, KD * ND)
    norm = np.broadcast_to(np.concatenate([g("q_norm_w"), g("kv_norm_w")])[None], (P, QR + KVR))
    rope = g("wq_rope").reshape(QR, H1, DR)
    halves = [rope[:, :, 0::2], rope[:, :, 1::2]]
    rope, swapped = np.concatenate(halves, 2), np.concatenate(halves[::-1], 2)
    kvup = g("wkv_up").reshape(KVR, H1, DN + DV)
    inv = f(1.0) / f(10000.0) ** (np.arange(0, DR, 2, dtype=f) / f(DR))
    angle = np.outer(np.arange(L, dtype=f), inv)
    c, s = np.cos(angle), np.sin(angle)
    cT, one = np.concatenate([c, c], 1).T, np.ones((DR, L), f)
    sT = np.concatenate([-s, s], 1).T
    rows = lambda t: t.reshape(TPB, P, DR // 2).transpose(1, 0, 2).reshape(P, P)
    tri = np.where(np.arange(P)[None] > np.arange(P)[:, None], f(-1e30), f(0))
    return {
        "la_down": down, "la_norm": norm, "la_rope": rope.reshape(QR, H1 * DR), "la_swapped": swapped.reshape(QR, H1 * DR),
        "la_qup": g("wq_up").reshape(QR, H1, DN).transpose(2, 1, 0).reshape(DN, H1 * QR),
        "la_kup": kvup[:, :, 0:DN].transpose(2, 1, 0).reshape(DN, H1 * KVR),
        "la_vup": kvup[:, :, DN:].transpose(2, 1, 0).reshape(DV, H1 * KVR),
        "la_wo": g("wo").reshape(H1, DV, D).transpose(1, 0, 2).reshape(DV, H1 * D),
        "la_cos": np.concatenate([np.concatenate([cT, one]), np.concatenate([one, cT])], 1),
        "la_sin": np.concatenate([sT, sT]), "la_kcos": rows(c), "la_ksin": rows(s),
        "la_mask": tri,
    }


def latent_loads(la, a, qup, kup, vup, wo):
    qw = la.qw[:, :].rearrange("p (c e n) -> p c e n", e=2, n=P)
    rope = a["la_rope"].rearrange("p (c e n) -> p c e n", e=2, n=DR)
    return [(qup, a["la_qup"]), (kup, a["la_kup"]), (vup, a["la_vup"]), (wo, a["la_wo"]),
            (qw[:, :, 0, 0:DR], rope[:, :, 0, :]), (qw[:, :, 1, KVR:P], rope[:, :, 1, :]),
            (la.qsw[:, :], a["la_swapped"]), (la.down[:, :], a["la_down"]), (la.norm[:, :], a["la_norm"]),
            (la.cos[:, :], a["la_cos"]), (la.sin[:, :], a["la_sin"]), (la.kcos[:, :], a["la_kcos"]),
            (la.ksin[:, :], a["la_ksin"]), (la.maskf[:, :], a["la_mask"])]


def ffn_layout(a):
    g = lambda n: np.asarray(a["L0_ffn_" + n])
    E, R = g("A_w").shape[0:2]
    main = np.concatenate([g("W_base"), g("W_router"), g("A_w").reshape(E * R, D)], 0).T
    return {"ff_main": main.reshape(KD, P, -1).transpose(1, 0, 2).reshape(P, -1),
            "ff_lora": g("B_w").transpose(0, 2, 1).reshape(E * R, D), "ff_bias": g("b_base")[None]}


def attention_layout(a):
    g = lambda n: np.asarray(a["L0_attn_" + n])
    w = np.stack([g("W" + c).T.reshape(KD, P, D) for c in "qkvo"], 1)
    return {"at_w": w.transpose(2, 0, 1, 3).reshape(P, -1), "at_lora_b": np.concatenate([g("B" + c) for c in "qkvo"], 1),
            "at_lora_a": np.concatenate([g("A" + c).T for c in "qkvo"], 1),
            "at_bias_qk": np.concatenate([g("bq").reshape(KD, P), g("bk").reshape(KD, P)]).T,
            "at_bias_v": np.broadcast_to(g("bv")[None], (P, D)), "at_bias_o": np.broadcast_to(g("bo")[None], (P, D))}


def moe_layout(a):
    g = lambda n: np.asarray(a["L1_ffn_" + n])
    half = lambda w: w.transpose(2, 0, 1).reshape(KD, P, NE, INTER)
    gu = np.concatenate([half(g("gate_weight")), half(g("up_weight"))], 3).transpose(1, 2, 0, 3).reshape(P, -1)
    cols = lambda t: t.reshape(TILES, P, TOPK).transpose(1, 0, 2).reshape(P, NC)
    return {"mo_w": np.concatenate([gu, g("down_weight").transpose(2, 0, 1).reshape(INTER, -1)], 1),
            "mo_idx": cols(g("topk_idx")), "mo_weight": cols(g("topk_weight"))}


def constants():
    f = np.float32
    return {"c_ident": np.eye(P, dtype=f), "c_iota": np.broadcast_to(np.arange(NBLK, dtype=f)[None], (P, NBLK)),
            "c_upper": np.triu(np.ones((P, P), f), 1),
            "c_token": (np.arange(P)[:, None] + P * (np.arange(NC) // TOPK)[None]).astype(np.int32)}


def program(nc, a, out):
    part_dram = nc.dram_tensor("part_dram", (B, 2, 3, D, L), BF16, kind="Internal").ap()
    max_dram = nc.dram_tensor("max_dram", (B, 3, 64, P), BF16, kind="Internal").ap()
    table_dram = nc.dram_tensor("table_dram", (P * NBLK, 1), I32, kind="Internal").ap()
    rows_dram = nc.dram_tensor("rows_dram", (B * L, D), F32, kind="Internal").ap()
    outs_dram = nc.dram_tensor("outs_dram", (NBLK * P, D), F32, kind="Internal").ap()
    with ExitStack() as ctx:
        def sb(n, shape, dt=F32):
            return ctx.enter_context(nc.sbuf_tensor(n, shape, dt))

        def sem(n):
            return ctx.enter_context(nc.semaphore(n))

        r = Rows(ctx, nc)
        ident, iota = sb("ident", [P, P]), sb("iota", [P, NBLK])
        slot, slot_token = sb("slot", [P, NC], I32), sb("slot_token", [P, NBLK], I32)
        block_expert, weight = sb("block_expert", [1, NBLK], I32), sb("weight", [P, NC])
        arena = sb("arena", [P, NE * (KD * 2 * INTER + D)])
        loaded, halved, experts_in, latent_in, written, spread = (sem(n) for n in (
            "loaded", "halved", "experts_in", "latent_in", "written", "spread"))
        EX = 8

        def start(loads):
            with nc.Block() as block:
                @block.sync
                def _(sp):
                    for dst, src in loads:
                        sp.dma_start(dst, src).then_inc(loaded, 16)
                    sp.wait_ge(loaded, 16 * len(loads))

                @block.vector
                def _(dve):
                    dve.wait_ge(loaded, 16 * len(loads))
                    dve.tensor_scalar(weight[:, :], weight[:, :], 0.5, None, ALU.mult).then_inc(halved, 1)
                    with dve.Fori(0, B) as b:
                        row_stats(dve, r, b)

        def load_experts():
            with nc.Block() as block:
                @block.sync
                def _(sp):
                    w = arena.shape[1] // EX
                    for c in range(EX):
                        sp.dma_start(arena[:, c * w:(c + 1) * w], a["mo_w"][:, c * w:(c + 1) * w]).then_inc(experts_in, 16)

        xv = out.rearrange("b (t p) d -> p (b t) d", p=P)
        with ExitStack() as c:
            fs = lambda n, shape, dt=F32: c.enter_context(nc.sbuf_tensor(n, shape, dt))
            wmain, wlora = fs("wmain", [P, a["ff_main"].shape[1]]), fs("wlora", [65, D])
            idx, token, upper = fs("idx", [P, NC], I32), fs("token", [P, NC], I32), fs("upper", [P, P])
            aw = fs("aw", [P, a["at_w"].shape[1]])
            alb, ala = fs("alb", [16, 4 * D]), fs("ala", [16, 4 * D])
            bqk, bv, bo = fs("bqk", [P, 4]), fs("bv", [P, D]), fs("bo", [P, D])
            start([(r.x[:, :].rearrange("p (t d) -> p t d", d=D), a["x"].rearrange("b (t p) d -> p (b t) d", p=P)),
                   (ident[:, :], a["c_ident"]), (iota[:, :], a["c_iota"]), (weight[:, :], a["mo_weight"]),
                   (wmain[:, :], a["ff_main"]), (wlora[0:64, :], a["ff_lora"]), (wlora[64:65, :], a["ff_bias"]),
                   (idx[:, :], a["mo_idx"]), (token[:, :], a["c_token"]), (upper[:, :], a["c_upper"]),
                   (aw[:, :], a["at_w"]), (alb[:, :], a["at_lora_b"]), (ala[:, :], a["at_lora_a"]),
                   (bqk[:, :], a["at_bias_qk"]), (bv[:, :], a["at_bias_v"]), (bo[:, :], a["at_bias_o"])])
            with nc.Block() as block:
                @block.vector
                def _(dve):
                    dve.tensor_scalar(wlora[64:65, :], wlora[64:65, :], 0.5, None, ALU.mult)
            with ExitStack() as c2:
                routing_stage(nc, idx, iota, upper, token, slot, block_expert, slot_token, table_dram, spread)
            ffn_stage(nc, "f1", r, ident, (wmain, wlora, iota))
            attention_stage(nc, r, ident, arena, aw, alb, ala, bqk, bv[:, :], bo[:, :], part_dram, max_dram)
            load_experts()
            ffn_stage(nc, "f2", r, ident, (wmain, wlora, iota))
        moe_stage(nc, "m1", r, ident, arena[:, :], (experts_in, 16 * EX), slot, weight, block_expert, slot_token,
                  rows_dram, outs_dram)
        with ExitStack() as c:
            la = Latent(c, nc)
            with ExitStack() as c2:
                raw = c2.enter_context(nc.sbuf_tensor("la_raw", [P, H1 * (QR + 2 * KVR + D)], F32))
                cut = np.cumsum([0, H1 * QR, H1 * KVR, H1 * KVR, H1 * D])
                qup, kup, vup, wo = (raw[:, int(cut[i]):int(cut[i + 1])] for i in range(4))
                latent_weights(nc, la, ident, qup, kup, vup, wo, latent_loads(la, a, qup, kup, vup, wo), latent_in)
            latent_stage(nc, r, ident, la)
        moe_stage(nc, "m2", r, ident, arena[:, :], (experts_in, 16 * EX), slot, weight, block_expert, slot_token,
                  rows_dram, outs_dram)
        with nc.Block() as block:
            @block.sync
            def _(sp):
                sp.dma_start(xv, r.x[:, :].rearrange("p (t d) -> p t d", d=D)).then_inc(written, 16)
                sp.wait_ge(written, 16)


def kernel(**inputs):
    import concourse.bacc as _bacc
    from concourse.bass_utils import run_bass_kernel_spmd as _run

    host = {"x": np.asarray(inputs["L0_attn_x"]), **ffn_layout(inputs), **attention_layout(inputs), **moe_layout(inputs),
            **latent_layout(inputs), **constants()}
    nc = _bacc.Bacc("TRN2", target_bir_lowering=False, num_devices=1)
    arrays, views = {}, {}
    for name, v in host.items():
        v = np.ascontiguousarray(v)
        arrays[f"in_{name}"] = v
        views[name] = nc.dram_tensor(f"in_{name}", v.shape, mybir.dt.from_np(v.dtype), kind="ExternalInput").ap()
    out = nc.dram_tensor("out_0", (B, L, D), F32, kind="ExternalOutput").ap()
    program(nc, views, out)
    return _run(nc, [arrays], core_ids=[0]).results[0]["out_0"]
```
